# Optimizing a Trainium2 kernel written in Bass

```python
import numpy as np
import jax
import jax.numpy as jnp

def _softmax(x, axis=-1):
    return jax.nn.softmax(x, axis=axis)

def _gelu(x):
    return jax.nn.gelu(x, approximate=True)

def _silu(x):
    return jax.nn.silu(x)

def _sigmoid(x):
    return jax.nn.sigmoid(x)

def _layernorm(x, axis=-1, eps=1e-05):
    m = jnp.mean(x, axis=axis, keepdims=True)
    v = jnp.var(x, axis=axis, keepdims=True)
    return (x - m) / jnp.sqrt(v + eps)

def _scatter_add(tgt, idx, src, axis=0):
    return tgt.at[idx].add(src)

def _segment_sum(src, seg, n):
    return jax.ops.segment_sum(src, seg, n)
kernel_name = 'mk_conv_preact_d2_conv_nchw64_r2_238195'

def setup_inputs(seed: int=0):
    np.random.seed(seed)
    _w = jnp.asarray

    def _rec_inputs():
        import jax
        import jax.numpy as jnp
        _gk = jax.random.key(seed)
        x = -0.0003929 + 0.9999 * jax.random.normal(jax.random.fold_in(_gk, 1), (4, 32, 128, 128), jnp.float32)
        return x
    x = _rec_inputs()

    def _L0_conv_setup():
        import jax, jax.numpy as jnp
        import numpy as np
        DIM = 32
        HID = 85
        P = 8

        def _forward(x, W_in, W_dw, fft_weight, W_out):
            B, C, H, W = x.shape
            xm = jnp.einsum('bchw,oc->bohw', x, W_in)
            x_spatial, x_freq, x_gate = jnp.split(xm, 3, axis=1)
            out_spatial = jax.lax.conv_general_dilated(x_spatial, W_dw, window_strides=(1, 1), padding='SAME', dimension_numbers=('NCHW', 'OIHW', 'NCHW'), feature_group_count=HID)
            h, w = (H // P, W // P)
            xp = x_freq.reshape(B, HID, h, P, w, P).transpose(0, 1, 2, 4, 3, 5)
            xf = jnp.fft.rfft2(xp)
            xf = xf * fft_weight
            xi = jnp.fft.irfft2(xf, s=(P, P))
            out_freq = xi.transpose(0, 1, 2, 4, 3, 5).reshape(B, HID, H, W)
            x_fused = jax.nn.gelu(x_gate, approximate=False) * (out_spatial + out_freq)
            return jnp.einsum('bchw,oc->bohw', x_fused, W_out)
        key = jax.random.key(seed)
        k1, k2, k3, k4 = jax.random.split(key, 4)
        x = jax.random.normal(k1, (4, DIM, 128, 128), dtype=jnp.float32)
        W_in = jax.random.normal(k2, (3 * HID, DIM), dtype=jnp.float32) * 0.05
        W_dw = jax.random.normal(k3, (HID, 1, 3, 3), dtype=jnp.float32) * 0.1
        fft_weight = jnp.ones((HID, 1, 1, P, P // 2 + 1), dtype=jnp.float32)
        W_out = jax.random.normal(k4, (DIM, HID), dtype=jnp.float32) * 0.05
        return {'x': x, 'W_in': W_in, 'W_dw': W_dw, 'fft_weight': fft_weight, 'W_out': W_out}
    _L0_conv_all = _L0_conv_setup()
    _L0_conv_in = {k: v for k, v in _L0_conv_all.items() if k in ('W_in', 'W_dw', 'fft_weight', 'W_out')}
    del _L0_conv_all

    def _L1_conv_setup():
        import jax, jax.numpy as jnp
        import numpy as np
        DIM = 32
        HID = 85
        P = 8

        def _forward(x, W_in, W_dw, fft_weight, W_out):
            B, C, H, W = x.shape
            xm = jnp.einsum('bchw,oc->bohw', x, W_in)
            x_spatial, x_freq, x_gate = jnp.split(xm, 3, axis=1)
            out_spatial = jax.lax.conv_general_dilated(x_spatial, W_dw, window_strides=(1, 1), padding='SAME', dimension_numbers=('NCHW', 'OIHW', 'NCHW'), feature_group_count=HID)
            h, w = (H // P, W // P)
            xp = x_freq.reshape(B, HID, h, P, w, P).transpose(0, 1, 2, 4, 3, 5)
            xf = jnp.fft.rfft2(xp)
            xf = xf * fft_weight
            xi = jnp.fft.irfft2(xf, s=(P, P))
            out_freq = xi.transpose(0, 1, 2, 4, 3, 5).reshape(B, HID, H, W)
            x_fused = jax.nn.gelu(x_gate, approximate=False) * (out_spatial + out_freq)
            return jnp.einsum('bchw,oc->bohw', x_fused, W_out)
        key = jax.random.key(seed)
        k1, k2, k3, k4 = jax.random.split(key, 4)
        x = jax.random.normal(k1, (4, DIM, 128, 128), dtype=jnp.float32)
        W_in = jax.random.normal(k2, (3 * HID, DIM), dtype=jnp.float32) * 0.05
        W_dw = jax.random.normal(k3, (HID, 1, 3, 3), dtype=jnp.float32) * 0.1
        fft_weight = jnp.ones((HID, 1, 1, P, P // 2 + 1), dtype=jnp.float32)
        W_out = jax.random.normal(k4, (DIM, HID), dtype=jnp.float32) * 0.05
        return {'x': x, 'W_in': W_in, 'W_dw': W_dw, 'fft_weight': fft_weight, 'W_out': W_out}
    _L1_conv_all = _L1_conv_setup()
    _L1_conv_in = {k: v for k, v in _L1_conv_all.items() if k in ('W_in', 'W_dw', 'fft_weight', 'W_out')}
    del _L1_conv_all
    return {'x': x, 'L0_conv_W_in': _L0_conv_in['W_in'], 'L0_conv_W_dw': _L0_conv_in['W_dw'], 'L0_conv_fft_weight': _L0_conv_in['fft_weight'], 'L0_conv_W_out': _L0_conv_in['W_out'], 'L1_conv_W_in': _L1_conv_in['W_in'], 'L1_conv_W_dw': _L1_conv_in['W_dw'], 'L1_conv_fft_weight': _L1_conv_in['fft_weight'], 'L1_conv_W_out': _L1_conv_in['W_out']}

def reference(x, L0_conv_W_in, L0_conv_W_dw, L0_conv_fft_weight, L0_conv_W_out, L1_conv_W_in, L1_conv_W_dw, L1_conv_fft_weight, L1_conv_W_out):
    import jax
    import jax.numpy as jnp

    def _L0_conv_ref(x, W_in, W_dw, fft_weight, W_out):
        import jax, jax.numpy as jnp
        import numpy as np
        DIM = 32
        HID = 85
        P = 8

        def _forward(x, W_in, W_dw, fft_weight, W_out):
            B, C, H, W = x.shape
            xm = jnp.einsum('bchw,oc->bohw', x, W_in)
            x_spatial, x_freq, x_gate = jnp.split(xm, 3, axis=1)
            out_spatial = jax.lax.conv_general_dilated(x_spatial, W_dw, window_strides=(1, 1), padding='SAME', dimension_numbers=('NCHW', 'OIHW', 'NCHW'), feature_group_count=HID)
            h, w = (H // P, W // P)
            xp = x_freq.reshape(B, HID, h, P, w, P).transpose(0, 1, 2, 4, 3, 5)
            xf = jnp.fft.rfft2(xp)
            xf = xf * fft_weight
            xi = jnp.fft.irfft2(xf, s=(P, P))
            out_freq = xi.transpose(0, 1, 2, 4, 3, 5).reshape(B, HID, H, W)
            x_fused = jax.nn.gelu(x_gate, approximate=False) * (out_spatial + out_freq)
            return jnp.einsum('bchw,oc->bohw', x_fused, W_out)
        return _forward(x, W_in, W_dw, fft_weight, W_out)

    def _L1_conv_ref(x, W_in, W_dw, fft_weight, W_out):
        import jax, jax.numpy as jnp
        import numpy as np
        DIM = 32
        HID = 85
        P = 8

        def _forward(x, W_in, W_dw, fft_weight, W_out):
            B, C, H, W = x.shape
            xm = jnp.einsum('bchw,oc->bohw', x, W_in)
            x_spatial, x_freq, x_gate = jnp.split(xm, 3, axis=1)
            out_spatial = jax.lax.conv_general_dilated(x_spatial, W_dw, window_strides=(1, 1), padding='SAME', dimension_numbers=('NCHW', 'OIHW', 'NCHW'), feature_group_count=HID)
            h, w = (H // P, W // P)
            xp = x_freq.reshape(B, HID, h, P, w, P).transpose(0, 1, 2, 4, 3, 5)
            xf = jnp.fft.rfft2(xp)
            xf = xf * fft_weight
            xi = jnp.fft.irfft2(xf, s=(P, P))
            out_freq = xi.transpose(0, 1, 2, 4, 3, 5).reshape(B, HID, H, W)
            x_fused = jax.nn.gelu(x_gate, approximate=False) * (out_spatial + out_freq)
            return jnp.einsum('bchw,oc->bohw', x_fused, W_out)
        return _forward(x, W_in, W_dw, fft_weight, W_out)

    def _gn(v, G=32, eps=1e-05):
        B_, C_, H_, W_ = v.shape
        g = v.reshape(B_, G, C_ // G, H_, W_)
        m = jnp.mean(g, axis=(2, 3, 4), keepdims=True)
        s = jnp.var(g, axis=(2, 3, 4), keepdims=True)
        return ((g - m) / jnp.sqrt(s + eps)).reshape(v.shape)

    def _ln_c(v, eps=1e-06):
        m = jnp.mean(v, axis=1, keepdims=True)
        s = jnp.var(v, axis=1, keepdims=True)
        return (v - m) / jnp.sqrt(s + eps)

    def _ln_t(v, eps=1e-05):
        m = jnp.mean(v, axis=-1, keepdims=True)
        s = jnp.var(v, axis=-1, keepdims=True)
        return (v - m) / jnp.sqrt(s + eps)

    def _to_tokens(v):
        B_, C_, H_, W_ = v.shape
        return v.reshape(B_, C_, H_ * W_).transpose(0, 2, 1)

    def _from_tokens(t, like):
        B_, C_, H_, W_ = like.shape
        return t.transpose(0, 2, 1).reshape(B_, C_, H_, W_)
    x = x + _L0_conv_ref(_gn(x), L0_conv_W_in, L0_conv_W_dw, L0_conv_fft_weight, L0_conv_W_out)
    x = x + _L1_conv_ref(_gn(x), L1_conv_W_in, L1_conv_W_dw, L1_conv_fft_weight, L1_conv_W_out)
    return x

_drawn_inputs = setup_inputs


def setup_inputs(seed=0):
    import zlib

    import numpy as np

    out = dict(_drawn_inputs(seed))
    spreads = {'L0_conv_fft_weight': (1.0, 0.6), 'L1_conv_fft_weight': (1.0, 0.6)}
    factors = {'L0_conv_W_dw': 8.0, 'L1_conv_W_dw': 8.0}
    for name, (base, spread) in spreads.items():
        noise = np.random.default_rng([zlib.crc32(name.encode()), seed]).standard_normal(out[name].shape)
        drawn = base * np.exp(spread * noise) if base else spread * noise
        out[name] = jnp.asarray(drawn.astype(out[name].dtype))
    for name, factor in factors.items():
        out[name] = (out[name] * factor).astype(out[name].dtype)
    return out
```

```python
from contextlib import ExitStack

import numpy as np

import concourse.bass as bass
import concourse.mybir as mybir

F32 = mybir.dt.float32
F16 = mybir.dt.float16
I32 = mybir.dt.int32
ALU = mybir.AluOpType
ACT = mybir.ActivationFunctionType
AX = mybir.AxisListType
RMAX = bass.bass_isa.ReduceOp.max

LAYERS = 2
B, C, H, W = 4, 32, 128, 128
HID = 85
P = 8
TH, TW = 8, 16
PIX = TH * TW
STRIPS = H // TH
TPS = W // TW
POS = STRIPS * TPS
SC = TH * (W + 2)
SW = TH * W
GC = B * HID
XS = 16.0
WS = 32.0
BS = 256.0
SS = XS * WS
UNROLL = 2 * TPS
EPS = 1e-5
MAIN, REST = 0, 1
PASSES = [(MAIN, -1), (MAIN, 0), (MAIN, 1), (MAIN, -1), (MAIN, 0), (MAIN, 1), (REST, -1), (REST, 1)]
NPASS = len(PASSES)
TAPS = 14
GROUPS = [[(0, -1, 0), (0, 0, 0), (0, 1, 0), (1, 0, 0)], [(1, -1, 0), (1, 1, 0), (1, -1, 1), (1, 1, 1)]]


def build(nc, x_in, w_in, w_dw, w_fft, w_out, basis, eye16, eye32, fold, y_out):
    ctx = ExitStack()
    with ctx:
        def sb(name, shape, dt=F32):
            return ctx.enter_context(nc.sbuf_tensor(name, shape, dt))

        def sem(name):
            return ctx.enter_context(nc.semaphore(name))

        x = sb("x", [128, H + 2, W])
        xn = sb("xn", [128, 2, TH + 2, W])
        parts = [sb(f"parts{i}", [128, 2, 3, SC], F16) for i in range(2)]
        stack = [sb(f"stack{i}", [128, 2, B, SC], F16) for i in range(2)]
        bas = sb("bas", [128, 4, 128], F16)
        id16 = sb("id16", [128, 128], F16)
        id32 = sb("id32", [128, 128])
        fold_sb = sb("fold_sb", [P * (P // 2 + 1), 128])
        win = sb("win", [128, 3 * HID])
        wdw = sb("wdw", [128, 9 * HID])
        fft = sb("fft", [P * (P // 2 + 1), HID])
        v32 = sb("v32", [128, 9, HID])
        vh = sb("vh", [128, 9, HID], F16)
        vl = sb("vl", [128, 9, HID], F16)
        wh = sb("wh", [128, 3 * HID], F16)
        wl = sb("wl", [128, 3 * HID], F16)
        amax = sb("amax", [128, 3])
        amaxr = sb("amaxr", [128, 3])
        m2 = sb("m2", [128, 2])
        p2 = sb("p2", [128, 2])
        ip2 = sb("ip2", [128, 2])
        cw = [sb(f"cw{i}", [128, NPASS, HID], F16) for i in range(LAYERS)]
        gw = [sb(f"gw{i}", [128, 2, HID], F16) for i in range(LAYERS)]
        fw = [sb(f"fw{i}", [128, 2, GC], F16) for i in range(LAYERS)]
        weff = [sb(f"weff{i}", [128, HID]) for i in range(LAYERS)]
        wo = [sb(f"wo{i}", [HID, C]) for i in range(LAYERS)]
        gsc = [sb(f"gsc{i}", [128, 1]) for i in range(LAYERS)]
        osc = [sb(f"osc{i}", [128, 1]) for i in range(LAYERS)]
        st = sb("st", [128, 2 * STRIPS, 6])
        mv = sb("mv", [128, 2])
        ve = sb("ve", [128, 1])
        sd = sb("sd", [128, 1])
        nr = sb("nr", [128, 4])
        rstd = sb("rstd", [128, 1])
        xt = sb("xt", [128, 2, 256], F16)
        fh = sb("fh", [128, 2, 128], F16)
        fl = sb("fl", [128, 2, 128], F16)
        g = sb("g", [128, 2, GC])
        y32 = sb("y32", [128, 2, GC])
        yh = sb("yh", [128, 2, GC], F16)
        yl = sb("yl", [128, 2, GC], F16)
        f = sb("f", [128, 2, GC])
        ft = sb("ft", [HID, 2, B * 128])

        def bank(name):
            return ctx.enter_context(nc.psum_tensor(name, [128, 512], F32))
        ps_s = [bank("ps_s0"), bank("ps_s1")]
        ps_g, ps_xt, ps_x, ps_z, ps_ft, ps_o = (bank(n) for n in ("ps_g", "ps_xt", "ps_x", "ps_z", "ps_ft", "ps_o"))

        s_const = sem("s_const")
        s_w = [sem(f"s_w{i}") for i in range(LAYERS)]
        s_wo = sem("s_wo")
        s_x = [sem(f"s_x{i}") for i in range(STRIPS)]
        s_zero = sem("s_zero")
        s_amax = sem("s_amax")
        s_all = sem("s_all")
        s_fold = sem("s_fold")
        s_chain = sem("s_chain")
        s_v = sem("s_v")
        s_tap = sem("s_tap")
        s_cw = sem("s_cw")
        s_var = sem("s_var")
        s_sd = sem("s_sd")
        s_xn = sem("s_xn")
        s_xh = sem("s_xh")
        s_xl = sem("s_xl")
        s_stk = [sem("s_stk0"), sem("s_stk1")]
        s_xtp = sem("s_xtp")
        s_xt = sem("s_xt")
        s_fp = sem("s_fp")
        s_fh = sem("s_fh")
        s_fl = sem("s_fl")
        s_z = sem("s_z")
        s_y = sem("s_y")
        s_yh = sem("s_yh")
        s_yl = sem("s_yl")
        s_gate = sem("s_gate")
        s_gelu = sem("s_gelu")
        s_s = sem("s_s")
        s_f = sem("s_f")
        s_ftp = sem("s_ftp")
        s_ft = sem("s_ft")
        s_o = sem("s_o")
        s_res = sem("s_res")
        s_out = sem("s_out")

        block = ctx.enter_context(nc.Block())

        def need(eng, semaphore, value):
            if not isinstance(value, int) or value > 0:
                eng.wait_ge(semaphore, value)

        LEAD = 4
        FIRST = 4
        ITERS = (POS - LEAD - FIRST) // UNROLL
        TAIL = FIRST + ITERS * UNROLL

        def schedule(eng, step):
            for i in range(-LEAD, FIRST):
                step(i, 0, True)
            with eng.Fori(0, ITERS) as it:
                for i in range(FIRST, FIRST + UNROLL):
                    step(i, it, False)
            for i in range(TAIL, POS + 2):
                step(i, 0, True)

        def live(i, offset, edge):
            return not edge or 0 <= i + offset < POS

        def staged(i):
            return i // TPS + 2, i % TPS - 4

        def store(sp, s):
            sp.wait_ge(s_res, (LAYERS - 1) * POS + (s + 1) * TPS)
            sp.dma_start(y_out[:, s * SW:(s + 1) * SW], x[:, 1 + TH * s:1 + TH * s + TH, :].rearrange("p r w -> p (r w)")).then_inc(s_out, 16)

        @block.sync
        def _(sp):
            def load_weights(l):
                if l:
                    sp.wait_ge(s_cw, l)
                for b in range(B):
                    sp.dma_start(win[C * b:C * b + C, :], w_in[l]).then_inc(s_w[l], 16)
                sp.dma_start(wdw[:, :], w_dw[l].partition_broadcast(128)).then_inc(s_w[l], 16)
                sp.dma_start(fft[:, :], w_fft[l]).then_inc(s_w[l], 16)

            load_weights(0)
            sp.dma_start(fold_sb[:, :], fold).then_inc(s_const, 16)
            sp.dma_start(bas[:, :, :], basis).then_inc(s_const, 16)
            sp.dma_start(id16[:, :], eye16).then_inc(s_const, 16)
            sp.dma_start(id32[:, :], eye32).then_inc(s_const, 16)
            for s in range(STRIPS):
                sp.dma_start(x[:, 1 + TH * s:1 + TH * s + TH, :].rearrange("p r w -> p (r w)"), x_in[:, s * SW:(s + 1) * SW]).then_inc(s_x[s], 16)
            for l in range(LAYERS):
                sp.dma_start(wo[l][:, :], w_out[l]).then_inc(s_wo, 16)
            load_weights(1)
            for l in range(LAYERS):
                for s in range(STRIPS):
                    need(sp, s_s, l * POS + (s - 1) * TPS)
                    sp.wait_ge(s_xh, 3 * (l * STRIPS + s + 1))
                    sp.wait_ge(s_xl, 3 * (l * STRIPS + s + 1))
                    for kind in (MAIN, REST):
                        for k, (part, dy, dx) in enumerate(GROUPS[kind]):
                            for b in range(B):
                                sp.dma_start(stack[s % 2][C * k:C * k + C, kind, b, 0:SC - TH * dx],
                                             parts[s % 2][C * b:C * b + C, part, 1 + dy, TH * dx:SC])\
                                    .then_inc(s_stk[s % 2], 16)
                    if l == LAYERS - 1 and s >= 2:
                        store(sp, s - 2)
            for s in (STRIPS - 2, STRIPS - 1):
                store(sp, s)
            sp.wait_ge(s_out, 16 * STRIPS)

        @block.tensor
        def _(pe):
            mm = nc.tensor.matmul
            pe.wait_ge(s_const, 64)
            for l in range(LAYERS):
                pe.wait_ge(s_w[l], 16 * (B + 2))
                need(pe, s_cw, l)
                mm(ps_z[:, 0:HID], fold_sb[:, :], fft[:, :], start=True, stop=True).then_inc(s_fold, 1)
            for l in range(LAYERS):
                pe.wait_ge(s_cw, l + 1)
                pe.wait_ge(s_tap, TAPS * (l + 1))
                pe.wait_ge(s_wo, 16 * LAYERS)
                base = l * POS

                def step(i, it, edge, l=l, base=base):
                    n = base + i + UNROLL * it
                    sk = stack[(i // TPS) % 2]
                    s = ps_s[i % 2]

                    def conv(b):
                        for m, (kind, dx) in enumerate(PASSES):
                            col = TH * (1 + TW * (i % TPS) + dx)
                            pix = sk[:, kind, b, col:col + PIX]
                            mm(s[:, HID * b:HID * (b + 1)], pix, cw[l][:, m, :],
                               start=(b == 0 and m == 0), stop=False)
                            if m == 1:
                                for part in range(2):
                                    gate = mm(ps_g[:, HID * b:HID * (b + 1)], pix, gw[l][:, part, :],
                                              start=(b == 0 and part == 0), stop=(b == B - 1 and part == 1))
                        if b == B - 1:
                            gate.then_inc(s_gate, 1)

                    if live(i, 0, edge):
                        if i % TPS == 0:
                            strips = l * (STRIPS // 2) + i // UNROLL + 1 + it
                            pe.wait_ge(s_stk[(i // TPS) % 2], strips * 16 * 8 * B)
                        need(pe, s_f, n - 1)
                        need(pe, s_gelu, n)
                        conv(0)
                    if live(i, 4, edge):
                        if (i + 4) % TPS == 0:
                            strips = l * STRIPS + (i + 4) // TPS + 1 + 2 * it
                            pe.wait_ge(s_xh, 3 * strips)
                            pe.wait_ge(s_xl, 3 * strips)
                        need(pe, s_xt, n + 4)
                        col = TH * (1 + TW * ((i + 4) % TPS))
                        for part in range(2):
                            t = mm(ps_xt[:, 128 * part:128 * part + 128],
                                   parts[((i + 4) // TPS) % 2][:, part, 1, col:col + PIX], id16[:, :],
                                   start=(part == 0), stop=(part == 1))
                        t.then_inc(s_xtp, 1)
                    if live(i, 0, edge):
                        conv(1)
                    if live(i, 3, edge):
                        k = (i + 3) % 2
                        need(pe, s_xt, n + 4)
                        need(pe, s_fh, n + 3)
                        need(pe, s_fl, n + 3)
                        mm(ps_x[:, 0:128], xt[:, k, 0:128], bas[:, 0, :], start=True, stop=False)
                        mm(ps_x[:, 0:128], xt[:, k, 0:128], bas[:, 1, :], start=False, stop=False)
                        mm(ps_x[:, 0:128], xt[:, k, 128:256], bas[:, 0, :], start=False, stop=True).then_inc(s_fp, 1)
                    if live(i, 0, edge):
                        conv(2)
                    if live(i, 2, edge):
                        k = i % 2
                        need(pe, s_fh, n + 3)
                        need(pe, s_fl, n + 3)
                        need(pe, s_y, n + 2)
                        mm(ps_z[:, 0:GC], fh[:, k, :], fw[l][:, 0, :], start=True, stop=False)
                        mm(ps_z[:, 0:GC], fh[:, k, :], fw[l][:, 1, :], start=False, stop=False)
                        mm(ps_z[:, 0:GC], fl[:, k, :], fw[l][:, 0, :], start=False, stop=True).then_inc(s_z, 1)
                    if live(i, 0, edge):
                        conv(3)
                        k = i % 2
                        need(pe, s_yh, n + 1)
                        mm(s[:, 0:GC], bas[:, 2, :], yh[:, k, :], start=False, stop=False)
                        mm(s[:, 0:GC], bas[:, 3, :], yh[:, k, :], start=False, stop=False)
                        need(pe, s_yl, n + 1)
                        mm(s[:, 0:GC], bas[:, 2, :], yl[:, k, :], start=False, stop=True).then_inc(s_s, 1)
                    if live(i, -1, edge):
                        k = (i - 1) % 2
                        need(pe, s_f, n)
                        need(pe, s_ft, n - 1)
                        for b in range(B):
                            t = nc.tensor.transpose(ps_ft[0:HID, b * 128:(b + 1) * 128],
                                                    f[:, k, HID * b:HID * (b + 1)], id32[:, :])
                        t.then_inc(s_ftp, 1)
                    if live(i, -2, edge):
                        k = i % 2
                        need(pe, s_ft, n - 1)
                        need(pe, s_res, n - 2)
                        for b in range(B):
                            o = mm(ps_o[C * b:C * b + C, 0:128], wo[l][:, :], ft[:, k, b * 128:(b + 1) * 128],
                                   start=True, stop=True)
                        o.then_inc(s_o, 1)

                schedule(pe, step)

        @block.scalar
        def _(act):
            for l in range(LAYERS):
                base = l * POS
                act.wait_ge(s_var, l + 1)
                nc.scalar.activation(sd[:, :], ve[:, :], ACT.Sqrt).then_inc(s_sd, 1)
                if l == 0:
                    act.wait_ge(s_zero, 6)

                def hi_part(s, it, dy, l=l):
                    act.wait_ge(s_xn, l * STRIPS + s + 2 * it + 1)
                    if dy == -1:
                        need(act, s_stk[s % 2], (l * (STRIPS // 2) + s // 2 + it) * 16 * 8 * B)
                        need(act, s_xtp, l * POS + (s - 1 + 2 * it) * TPS)
                    nc.scalar.activation(
                        parts[s % 2][:, 0, 1 + dy, TH:TH + SW].rearrange("p (w r) -> p w r", r=TH),
                        xn[:, s % 2, 1 + dy:1 + dy + TH, :].rearrange("p r w -> p w r"),
                        ACT.Copy).then_inc(s_xh, 1)

                for dy in (-1, 0, 1):
                    hi_part(0, 0, dy)

                def step(i, it, edge, l=l, base=base):
                    n = base + i + UNROLL * it
                    if live(i, 4, edge):
                        need(act, s_xtp, n + 5)
                        need(act, s_fp, n + 3)
                        nc.scalar.activation(xt[:, i % 2, :], ps_xt[:, 0:256], ACT.Copy).then_inc(s_xt, 1)
                    if live(i, 3, edge):
                        need(act, s_fp, n + 4)
                        need(act, s_z, n + 2)
                        nc.scalar.activation(fh[:, (i + 3) % 2, :], ps_x[:, 0:128], ACT.Copy,
                                             scale=1.0 / BS).then_inc(s_fh, 1)
                    if live(i, 0, edge):
                        need(act, s_gate, n + 1)
                        need(act, s_f, n - 1)
                        nc.scalar.activation(g[:, i % 2, :], ps_g[:, 0:GC], ACT.Gelu,
                                             scale=gsc[l][:, 0:1]).then_inc(s_gelu, 1)
                    if live(i, 2, edge):
                        need(act, s_y, n + 3)
                        need(act, s_s, n + 1)
                        nc.scalar.activation(yh[:, i % 2, :], y32[:, i % 2, :], ACT.Copy).then_inc(s_yh, 1)
                    if live(i, -1, edge):
                        need(act, s_ftp, n)
                        need(act, s_o, n - 2)
                        nc.scalar.activation(ft[:, (i - 1) % 2, :], ps_ft[0:HID, 0:B * 128],
                                             ACT.Copy).then_inc(s_ft, 1)
                    s, k = staged(i)
                    if 0 <= k < 3 and (not edge or s < STRIPS):
                        hi_part(s, it, k - 1)
                act.wait_ge(s_cw, l + 1)
                schedule(act, step)

        @block.gpsimd
        def _(pool):
            for l in range(LAYERS):
                pool.wait_ge(s_amax, l + 1)
                nc.gpsimd.partition_all_reduce(amaxr[:, :], amax[:, :], 128, RMAX).then_inc(s_all, 1)
                pool.wait_ge(s_v, l + 1)
                for m0, part in ((0, vh), (3, vl)):
                    for k, (_, dy, _) in enumerate(GROUPS[MAIN]):
                        rows = slice(C * k, C * k + C)
                        nc.gpsimd.tensor_copy(cw[l][rows, m0:m0 + 3, :],
                                              part[rows, 3 * dy + 3:3 * dy + 6, :]).then_inc(s_tap, 1)
                for m in (6, 7):
                    for k, (_, dy, gx) in enumerate(GROUPS[REST]):
                        tap = PASSES[m][1] + gx
                        if abs(tap) > 1:
                            continue
                        rows = slice(C * k, C * k + C)
                        nc.gpsimd.tensor_copy(cw[l][rows, m, :], vh[rows, 3 * dy + 3 + tap + 1, :]).then_inc(s_tap, 1)
                pool.wait_ge(s_tap, TAPS * (l + 1))
            for l in range(LAYERS):
                base = l * POS

                def step(i, it, edge, base=base):
                    n = base + i + UNROLL * it
                    if live(i, 2, edge):
                        k = i % 2
                        need(pool, s_yh, n + 3)
                        need(pool, s_s, n + 1)
                        nc.gpsimd.tensor_tensor(yl[:, k, :], y32[:, k, :], yh[:, k, :],
                                                ALU.subtract).then_inc(s_yl, 1)
                schedule(pool, step)

        @block.vector
        def _(dve):
            links = [0]
            v = nc.vector

            def link(ins):
                links[0] += 1
                ins.then_inc(s_chain, 1)
                dve.wait_ge(s_chain, links[0])

            for i in range(2):
                v.memset(parts[i][:, :, :, 0:TH], 0.0).then_inc(s_zero, 1)
                v.memset(parts[i][:, :, :, SC - TH:SC], 0.0).then_inc(s_zero, 1)
                v.memset(stack[i][:, REST, :, SC - TH:SC], 0.0).then_inc(s_zero, 1)
            v.memset(x[:, 0, :], 0.0)
            v.memset(x[:, H + 1, :], 0.0)

            def prepare(l):
                v.memset(cw[l][:, :, :], 0.0)
                v.memset(gw[l][:, :, :], 0.0)
                v.memset(fw[l][:, :, :], 0.0)
                link(v.memset(amax[:, :], 0.0))
                dve.wait_ge(s_w[l], 16 * (B + 2))
                v.tensor_reduce(amax[:, 0:1], win[:, :], AX.X, ALU.max, apply_absolute_value=True)
                v.tensor_reduce(amax[:, 1:2], wdw[:, :], AX.X, ALU.max, apply_absolute_value=True)
                v.tensor_reduce(amax[0:40, 2:3], fft[:, :], AX.X, ALU.max,
                                apply_absolute_value=True).then_inc(s_amax, 1)
                dve.wait_ge(s_all, l + 1)
                v.tensor_scalar(m2[:, 0:1], amaxr[:, 0:1], 1e-30, None, ALU.max)
                link(v.scalar_tensor_tensor(m2[:, 1:2], amaxr[:, 1:2], 1e-30, amaxr[:, 2:3], ALU.max, ALU.max))
                link(v.tensor_scalar(p2[:, :].bitcast(I32), m2[:, :].bitcast(I32), 0x7F800000, None,
                                     ALU.bitwise_and))
                link(v.reciprocal(ip2[:, :], p2[:, :]))
                v.tensor_scalar(gsc[l][:, :], p2[:, 0:1], 1.0 / SS, None, ALU.mult)
                v.tensor_scalar(osc[l][:, :], p2[:, 0:1], p2[:, 1:2], 1.0 / SS, ALU.mult, ALU.mult)
                v.tensor_scalar(win[:, :], win[:, :], ip2[:, 0:1], WS, ALU.mult, ALU.mult)
                link(v.tensor_scalar(wdw[:, :], wdw[:, :], ip2[:, 1:2], None, ALU.mult))
                dve.wait_ge(s_fold, l + 1)
                v.tensor_scalar(weff[l][:, :], ps_z[:, 0:HID], ip2[:, 1:2], 1.0 / BS, ALU.mult, ALU.mult)
                v.tensor_copy(wh[:, :], win[:, :])
                link(v.tensor_tensor(v32[:, :, :], wdw[:, :].rearrange("p (t o) -> p t o", t=9),
                                     win[:, None, 0:HID].broadcast_to([128, 9, HID]), ALU.mult))
                v.tensor_tensor(wl[:, :], win[:, :], wh[:, :], ALU.subtract)
                link(v.tensor_copy(vh[:, :, :], v32[:, :, :]))
                v.tensor_tensor(vl[:, :, :], v32[:, :, :], vh[:, :, :], ALU.subtract).then_inc(s_v, 1)
                for part, src in enumerate((wh, wl)):
                    for group in (1, 3):
                        rows = slice(C * group, C * group + C)
                        v.tensor_copy(gw[l][rows, part, :], src[rows, 2 * HID:3 * HID])
                    for b in range(B):
                        rows = slice(C * b, C * b + C)
                        last = v.tensor_copy(fw[l][rows, part, HID * b:HID * b + HID], src[rows, HID:2 * HID])
                last.then_inc(s_cw, 1)

            def strip_stats(s, it=0):
                for h in range(2):
                    row = 1 + TH * s + TH // 2 * h + 2 * TH * it
                    last = v.bn_stats(st[:, bass.ds(2 * s + h + 4 * it, 1), :].rearrange("p a b -> p (a b)"),
                                      x[:, bass.ds(row, TH // 2), :].rearrange("p r w -> p (r w)"))
                return last

            prepare(0)
            for s in range(STRIPS):
                dve.wait_ge(s_x[s], 16)
                last = strip_stats(s)
            link(last)
            for l in range(LAYERS):
                base = l * POS
                link(v.bn_aggr(mv[:, :], st[:, :, :].rearrange("p a b -> p (a b)")))
                link(v.tensor_scalar(ve[:, :], mv[:, 1:2], EPS, None, ALU.add))
                v.memset(nr[:, 3:4], 0.0).then_inc(s_var, 1)
                dve.wait_ge(s_sd, l + 1)
                link(v.reciprocal(nr[:, 0:1], sd[:, :]))
                link(v.tensor_scalar(nr[:, 1:2], nr[:, 0:1], nr[:, 0:1], ve[:, 0:1], ALU.mult, ALU.mult))
                link(v.tensor_scalar(nr[:, 2:3], nr[:, 1:2], -0.5, 1.5, ALU.mult, ALU.add))
                link(v.tensor_scalar(rstd[:, :], nr[:, 2:3], nr[:, 0:1], XS, ALU.mult, ALU.mult))

                for row in (0, H + 1):
                    last = v.tensor_scalar(x[:, row, :], x[:, row, :], 0.0, mv[:, 0:1], ALU.mult, ALU.add)
                link(last)

                def norm(s, it, l=l):
                    need(dve, s_xl, 3 * (l * STRIPS + s - 1 + 2 * it))
                    v.tensor_scalar(xn[:, s % 2, :, :], x[:, bass.ds(TH * s + 2 * TH * it, TH + 2), :], mv[:, 0:1],
                                    rstd[:, 0:1], ALU.subtract, ALU.mult).then_inc(s_xn, 1)

                def lo_part(s, it, dy, l=l):
                    dve.wait_ge(s_xh, 3 * (l * STRIPS + s + 2 * it) + dy + 2)
                    part = parts[s % 2][:, :, 1 + dy, TH:TH + SW].rearrange("p a (w r) -> p a w r", r=TH)
                    v.tensor_tensor(part[:, 1], xn[:, s % 2, 1 + dy:1 + dy + TH, :].rearrange("p r w -> p w r"),
                                    part[:, 0], ALU.subtract).then_inc(s_xl, 1)

                norm(0, 0)
                for dy in (-1, 0, 1):
                    lo_part(0, 0, dy)
                if l == 0:
                    prepare(1)

                def step(i, it, edge, l=l, base=base):
                    n = base + i + UNROLL * it
                    if live(i, -1, edge):
                        k = (i - 1) % 2
                        need(dve, s_s, n)
                        need(dve, s_gelu, n)
                        if l + 1 < LAYERS and i % TPS == 2:
                            need(dve, s_res, n - 2)
                        need(dve, s_ftp, n - 2)
                        v.tensor_tensor(f[:, k, :], ps_s[k][:, 0:GC], g[:, k, :], ALU.mult).then_inc(s_f, 1)
                        if l + 1 < LAYERS and i % TPS == 2 and i > TPS:
                            strip_stats(i // TPS - 1, it)
                    if live(i, 3, edge):
                        k = (i + 3) % 2
                        need(dve, s_fh, n + 4)
                        need(dve, s_z, n + 2)
                        v.scalar_tensor_tensor(fl[:, k, :], ps_x[:, 0:128], 1.0 / BS, fh[:, k, :],
                                               ALU.mult, ALU.subtract).then_inc(s_fl, 1)
                    if live(i, 2, edge):
                        k = i % 2
                        need(dve, s_z, n + 3)
                        need(dve, s_yl, n + 1)
                        v.tensor_tensor(y32[:, k, :].rearrange("p (b o) -> p b o", b=B),
                                        ps_z[:, 0:GC].rearrange("p (b o) -> p b o", b=B),
                                        weff[l][:, None, :].broadcast_to([128, B, HID]),
                                        ALU.mult).then_inc(s_y, 1)
                    if live(i, -2, edge):
                        q = i - 2
                        need(dve, s_o, n - 1)
                        xv = x[:, bass.ds(1 + TH * (q // TPS) + 2 * TH * it, TH),
                               TW * (q % TPS):TW * (q % TPS) + TW].rearrange("p r w -> p w r")
                        v.scalar_tensor_tensor(xv, ps_o[:, 0:128].rearrange("p (w r) -> p w r", r=TH),
                                               osc[l][:, 0:1], xv, ALU.mult, ALU.add).then_inc(s_res, 1)
                    s, k = staged(i)
                    if k >= 0 and (not edge or s < STRIPS):
                        if k == 0:
                            norm(s, it)
                        else:
                            lo_part(s, it, k - 2)
                schedule(dve, step)
                if l + 1 < LAYERS:
                    dve.wait_ge(s_res, base + POS)
                    link(strip_stats(STRIPS - 1))


def fourier():
    yy, xx = np.meshgrid(np.arange(P), np.arange(P), indexing="ij")
    comps, sources, seen = [], [], set()
    for kh in range(P):
        for kw in range(P // 2 + 1):
            if (kh, kw) in seen:
                continue
            mirror = ((-kh) % P, (-kw) % P)
            seen |= {(kh, kw), mirror}
            theta = 2 * np.pi * (kh * yy + kw * xx) / P
            src = [(kh, kw), mirror] if kw in (0, P // 2) else [(kh, kw)]
            if mirror == (kh, kw):
                comps.append(np.cos(theta) / P)
                sources.append(src[:1])
            else:
                for wave in (np.cos(theta), np.sin(theta)):
                    comps.append(wave * np.sqrt(2) / P)
                    sources.append(src)
    assert len(comps) == P * P
    return np.stack([c.reshape(-1) for c in comps], 1), sources


def constants():
    basis, sources = fourier()
    full = np.zeros((PIX, PIX))
    for pix in range(PIX):
        c, r = divmod(pix, TH)
        full[pix, (c // P) * P * P:(c // P + 1) * P * P] = basis[r * P + c % P]
    full *= BS
    packed = np.zeros((128, 4, 128), np.float16)
    for k, m in enumerate((full, full.T)):
        packed[:, 2 * k] = m.astype(np.float16)
        packed[:, 2 * k + 1] = (m - packed[:, 2 * k].astype(np.float64)).astype(np.float16)
    fold = np.zeros((P * (P // 2 + 1), 128), np.float32)
    for k, src in enumerate(sources):
        for kh, kw in src:
            fold[kh * (P // 2 + 1) + kw, [k, P * P + k]] += 1.0 / len(src)
    return {"basis": packed, "eye16": np.eye(128, dtype=np.float16), "eye32": np.eye(128, dtype=np.float32),
            "fold": fold}


def kernel(**inputs):
    import concourse.bacc as bacc
    from concourse.bass_utils import run_bass_kernel_spmd

    arrays = {"x": np.ascontiguousarray(np.asarray(inputs["x"]).reshape(B * C, H * W))}
    for l in range(LAYERS):
        raw = {k: np.asarray(inputs[f"L{l}_conv_{k}"]) for k in ("W_in", "W_dw", "fft_weight", "W_out")}
        arrays[f"w_in{l}"] = np.ascontiguousarray(raw["W_in"].T)
        arrays[f"w_dw{l}"] = np.ascontiguousarray(raw["W_dw"].reshape(HID, 9).T.reshape(9 * HID))
        arrays[f"w_fft{l}"] = np.ascontiguousarray(raw["fft_weight"].reshape(HID, -1).T)
        arrays[f"w_out{l}"] = np.ascontiguousarray(raw["W_out"].T)
    arrays.update(constants())

    nc = bacc.Bacc("TRN2", target_bir_lowering=False, num_devices=1)
    ap = {k: nc.dram_tensor("in_" + k, a.shape, mybir.dt.from_np(a.dtype), kind="ExternalInput").ap()
          for k, a in arrays.items()}
    y = nc.dram_tensor("out_y", (B * C, H * W), F32, kind="ExternalOutput").ap()
    per_layer = [[ap[f"{k}{l}"] for l in range(LAYERS)] for k in ("w_in", "w_dw", "w_fft", "w_out")]
    build(nc, ap["x"], *per_layer, ap["basis"], ap["eye16"], ap["eye32"], ap["fold"], y)
    got = run_bass_kernel_spmd(nc, [{"in_" + k: a for k, a in arrays.items()}], core_ids=[0])
    return got.results[0]["out_y"].reshape(B, C, H, W)
```

```python
from contextlib import ExitStack

import numpy as np

import concourse.bass as bass
import concourse.mybir as mybir

F32 = mybir.dt.float32
F16 = mybir.dt.float16
I32 = mybir.dt.int32
ALU = mybir.AluOpType
ACT = mybir.ActivationFunctionType
AX = mybir.AxisListType
RMAX = bass.bass_isa.ReduceOp.max

LAYERS = 2
B, C, H, W = 4, 32, 128, 128
HID = 85
P = 8
TH, TW = 8, 16
PIX = TH * TW
STRIPS = H // TH
TPS = W // TW
POS = STRIPS * TPS
SC = TH * (W + 2)
SW = TH * W
GC = B * HID
XS = 16.0
WS = 32.0
BS = 256.0
SS = XS * WS
UNROLL = 2 * TPS
EPS = 1e-5
MAIN, ALT, GATE, THIRD = range(4)
STACKS = 4
HI_ORDER = (-1, 0, 1)
LO_ORDER = (-1, 0, 1)
PASSES = [(MAIN, -1), (MAIN, 0), (MAIN, 1), (ALT, -1), (ALT, 0), (ALT, 1), (THIRD, -1)]
NPASS = len(PASSES)
TAPS = 14
GROUPS = [(0, slice(MAIN, ALT + 1), 0, -1, 0), (1, slice(MAIN, GATE + 1), 0, 0, 0), (2, slice(MAIN, ALT + 1), 0, 1, 0),
          (0, slice(GATE, GATE + 1), 0, 0, 0), (3, slice(MAIN, GATE + 1, 2), 1, 0, 0),
          (3, slice(ALT, ALT + 1), 1, 1, 0), (0, slice(THIRD, THIRD + 1), 1, -1, 0),
          (1, slice(THIRD, THIRD + 1), 1, -1, 1), (2, slice(THIRD, THIRD + 1), 1, -1, 2)]
LOADS = [(b, group) for group in GROUPS for b in range(B)]
BY_COPY = [(b, group) for b, group in LOADS if GROUPS.index(group) in (5, 7, 8)]
COPY_STEPS = 4
BY_DMA = [load for load in LOADS if load not in BY_COPY]
SHARED = BY_DMA[1::3] + BY_DMA[8::9]
BY_SP = [load for load in BY_DMA if load not in SHARED]


def build(nc, x_in, w_in, w_dw, w_fft, w_out, basis, eye16, eye32, fold, y_out):
    ctx = ExitStack()
    with ctx:
        def sb(name, shape, dt=F32):
            return ctx.enter_context(nc.sbuf_tensor(name, shape, dt))

        def sem(name):
            return ctx.enter_context(nc.semaphore(name))

        x = sb("x", [128, H + 2, W])
        xn = sb("xn", [128, TH + 2, W])
        parts = [sb(f"parts{i}", [128, 2, 3, SC], F16) for i in range(2)]
        stack = [sb(f"stack{i}", [128, STACKS, B, SC], F16) for i in range(2)]
        bas = sb("bas", [128, 4, 128], F16)
        id16 = sb("id16", [128, 128], F16)
        id32 = sb("id32", [128, 128])
        fold_sb = sb("fold_sb", [P * (P // 2 + 1), 128])
        win = [sb(f"win{i}", [128, 3 * HID]) for i in range(LAYERS)]
        wdw = [sb(f"wdw{i}", [128, 9 * HID]) for i in range(LAYERS)]
        fft = [sb(f"fft{i}", [P * (P // 2 + 1), HID]) for i in range(LAYERS)]
        vh = sb("vh", [128, 9, HID], F16)
        vl = sb("vl", [128, 9, HID], F16)
        wh = sb("wh", [128, 3 * HID], F16)
        wl = sb("wl", [128, 3 * HID], F16)
        amax = sb("amax", [128, 3, LAYERS])
        amaxr = sb("amaxr", [128, 3, LAYERS])
        tops = sb("tops", [128, 2, LAYERS])
        p2 = sb("p2", [128, 2, LAYERS])
        ip2 = sb("ip2", [128, 2, LAYERS])
        cw = [sb(f"cw{i}", [128, NPASS, HID], F16) for i in range(LAYERS)]
        gw = [sb(f"gw{i}", [128, HID], F16) for i in range(LAYERS)]
        fw = [sb(f"fw{i}", [128, 2, GC], F16) for i in range(LAYERS)]
        weff = [sb(f"weff{i}", [128, HID]) for i in range(LAYERS)]
        wo = [sb(f"wo{i}", [HID, C]) for i in range(LAYERS)]
        gsc = [sb(f"gsc{i}", [128, 1]) for i in range(LAYERS)]
        osc = [sb(f"osc{i}", [128, 1]) for i in range(LAYERS)]
        st = sb("st", [128, 2 * STRIPS, 6])
        mv = sb("mv", [128, 2])
        ve = sb("ve", [128, 1])
        power = sb("power", [128, 1])
        nr = sb("nr", [128, 4])
        rstd = sb("rstd", [128, 1])
        xt = sb("xt", [128, 2, 256], F16)
        fh = sb("fh", [128, 2, 128], F16)
        fl = sb("fl", [128, 2, 128], F16)
        g = sb("g", [128, 2, GC])
        y32 = sb("y32", [128, 2, GC])
        yh = sb("yh", [128, 2, GC], F16)
        yl = sb("yl", [128, 2, GC], F16)
        f = sb("f", [128, 2, GC])
        ft = sb("ft", [HID, 2, B * 128])

        def bank(name):
            return ctx.enter_context(nc.psum_tensor(name, [128, 512], F32))
        ps_s = [bank("ps_s0"), bank("ps_s1")]
        ps_g, ps_xt, ps_x, ps_z, ps_ft, ps_o = (bank(n) for n in ("ps_g", "ps_xt", "ps_x", "ps_z", "ps_ft", "ps_o"))

        s_const = sem("s_const")
        s_w = [sem(f"s_w{i}") for i in range(LAYERS)]
        s_wo = sem("s_wo")
        s_x = [sem(f"s_x{i}") for i in range(STRIPS)]
        s_zero = sem("s_zero")
        s_amax = sem("s_amax")
        s_all = sem("s_all")
        s_fold = sem("s_fold")
        s_chain = sem("s_chain")
        s_ready = sem("s_ready")
        s_scaled = sem("s_scaled")
        s_v32 = sem("s_v32")
        s_wh = sem("s_wh")
        s_wl = sem("s_wl")
        s_vh = sem("s_vh")
        s_cw = sem("s_cw")
        s_var = sem("s_var")
        s_root = sem("s_root")
        s_power = sem("s_power")
        s_xn = sem("s_xn")
        s_xh = sem("s_xh")
        s_xl = sem("s_xl")
        s_stk = [sem(f"s_stk{i}") for i in range(2)]
        s_first = sem("s_first")
        s_copy = sem("s_copy")
        s_xtp = sem("s_xtp")
        s_xt = sem("s_xt")
        s_fp = sem("s_fp")
        s_fh = sem("s_fh")
        s_fl = sem("s_fl")
        s_z = sem("s_z")
        s_y = sem("s_y")
        s_yh = sem("s_yh")
        s_yl = sem("s_yl")
        s_gate = sem("s_gate")
        s_gelu = sem("s_gelu")
        s_s = sem("s_s")
        s_f = sem("s_f")
        s_ftp = sem("s_ftp")
        s_ft = sem("s_ft")
        s_o = sem("s_o")
        s_res = sem("s_res")
        s_out = sem("s_out")

        block = ctx.enter_context(nc.Block())

        def need(eng, semaphore, value):
            if not isinstance(value, int) or value > 0:
                eng.wait_ge(semaphore, value)

        LEAD = 4
        FIRST = 4
        ITERS = (POS - LEAD - FIRST) // UNROLL
        TAIL = FIRST + ITERS * UNROLL

        def schedule(eng, step):
            for i in range(-LEAD, FIRST):
                step(i, 0, True)
            with eng.Fori(0, ITERS) as it:
                for i in range(FIRST, FIRST + UNROLL):
                    step(i, it, False)
            for i in range(TAIL, POS + 2):
                step(i, 0, True)

        def live(i, offset, edge):
            return not edge or 0 <= i + offset < POS

        def staged(i):
            return i // TPS + 2, i % TPS - 4

        def group_ap(s, load):
            b, (k, kinds, part, dy, dx) = load
            dst = stack[s % 2][C * k:C * k + C, kinds, b, 0:SC - TH * dx]
            src = parts[s % 2][C * b:C * b + C, part, 1 + dy, TH * dx:SC]
            return dst, src[:, None, :].broadcast_to([C, len(range(*kinds.indices(STACKS))), SC - TH * dx])

        def load_stacks(eng, l, s, loads, loaded):
            need(eng, s_s, l * POS + (s - 1) * TPS)
            waited = None
            for load in loads:
                part, dy = load[1][2:4]
                if (part, dy) != waited:
                    waited = (part, dy)
                    eng.wait_ge((s_xh, s_xl)[part], 3 * (l * STRIPS + s) + (HI_ORDER, LO_ORDER)[part].index(dy) + 1)
                dst, src = group_ap(s, load)
                eng.dma_start(dst, src).then_inc(loaded, 16)

        def store(sp, s):
            sp.wait_ge(s_res, (LAYERS - 1) * POS + (s + 1) * TPS)
            sp.dma_start(y_out[:, s * SW:(s + 1) * SW], x[:, 1 + TH * s:1 + TH * s + TH, :].rearrange("p r w -> p (r w)")).then_inc(s_out, 16)

        def load_weights(eng, l):
            for b in range(B):
                eng.dma_start(win[l][C * b:C * b + C, :], w_in[l]).then_inc(s_w[l], 16)
            eng.dma_start(wdw[l][:, :], w_dw[l].partition_broadcast(128)).then_inc(s_w[l], 16)
            eng.dma_start(fft[l][:, :], w_fft[l]).then_inc(s_w[l], 16)

        @block.sync
        def _(sp):
            load_weights(sp, 0)
            sp.dma_start(fold_sb[:, :], fold).then_inc(s_const, 16)
            sp.dma_start(bas[:, :, :], basis).then_inc(s_const, 16)
            sp.dma_start(id16[:, :], eye16).then_inc(s_const, 16)
            sp.dma_start(id32[:, :], eye32).then_inc(s_const, 16)
            for s in range(STRIPS):
                sp.dma_start(x[:, 1 + TH * s:1 + TH * s + TH, :].rearrange("p r w -> p (r w)"), x_in[:, s * SW:(s + 1) * SW]).then_inc(s_x[s], 16)
            for l in range(LAYERS):
                sp.dma_start(wo[l][:, :], w_out[l]).then_inc(s_wo, 16)
            for l in range(LAYERS):
                for s in range(STRIPS):
                    load_stacks(sp, l, s, BY_DMA if s else BY_SP, s_stk[s % 2])
                    if l == LAYERS - 1 and s >= 2:
                        store(sp, s - 2)
            for s in (STRIPS - 2, STRIPS - 1):
                store(sp, s)
            sp.wait_ge(s_out, 16 * STRIPS)

        @block.tensor
        def _(pe):
            mm = nc.tensor.matmul
            pe.wait_ge(s_const, 64)
            for l in range(LAYERS):
                pe.wait_ge(s_w[l], 16 * (B + 2))
                mm((ps_x, ps_ft)[l][:, 0:HID], fold_sb[:, :], fft[l][:, :], start=True, stop=True).then_inc(s_fold, 1)
            for l in range(LAYERS):
                base = l * POS

                def step(i, it, edge, l=l, base=base):
                    n = base + i + UNROLL * it
                    sk = stack[(i // TPS) % 2]

                    s = ps_s[i % 2]

                    def pixels(kind, b, dx, rows=128):
                        col = TH * (1 + TW * (i % TPS) + dx)
                        return sk[0:rows, kind, b, col:col + PIX]

                    def conv(b):
                        for m, (kind, dx) in enumerate(PASSES):
                            rows = 3 * C if kind == THIRD else 128
                            mm(s[:, HID * b:HID * (b + 1)], pixels(kind, b, dx, rows), cw[l][0:rows, m, :],
                               start=(b == 0 and m == 0), stop=False)
                        gate = mm(ps_g[:, HID * b:HID * (b + 1)], pixels(GATE, b, 0), gw[l][:, :],
                                  start=(b == 0), stop=(b == B - 1))
                        if b == B - 1:
                            gate.then_inc(s_gate, 1)

                    def stacks_loaded():
                        odd = (i // TPS) % 2
                        strips = l * (STRIPS // 2) + i // UNROLL + 1 + it
                        shared = 0 if odd else (l + 1) * 16 * len(SHARED)
                        pe.wait_ge(s_stk[odd], strips * (16 * len(BY_DMA)) - shared)
                        if i == 0:
                            pe.wait_ge(s_first, (l + 1) * 16 * len(SHARED))
                        pe.wait_ge(s_copy, (l * STRIPS + i // TPS + 1 + 2 * it) * len(BY_COPY))

                    if live(i, 0, edge):
                        need(pe, s_f, n - 1)
                        need(pe, s_gelu, n)
                        if i % TPS == 0:
                            stacks_loaded()
                        if i == 0:
                            pe.wait_ge(s_ready, TAPS * (l + 1))
                            pe.wait_ge(s_wo, 16 * LAYERS)
                        conv(0)
                    if live(i, 4, edge):
                        if (i + 4) % TPS == 0:
                            strips = l * STRIPS + (i + 4) // TPS + 1 + 2 * it
                            pe.wait_ge(s_xh, 3 * strips)
                            pe.wait_ge(s_xl, 3 * strips)
                        need(pe, s_xt, n + 4)
                        col = TH * (1 + TW * ((i + 4) % TPS))
                        for part in range(2):
                            t = mm(ps_xt[:, 128 * part:128 * part + 128],
                                   parts[((i + 4) // TPS) % 2][:, part, 1, col:col + PIX], id16[:, :],
                                   start=(part == 0), stop=(part == 1))
                        t.then_inc(s_xtp, 1)
                    if live(i, 0, edge):
                        conv(1)
                    if live(i, 3, edge):
                        k = (i + 3) % 2
                        need(pe, s_xt, n + 4)
                        need(pe, s_fh, n + 3)
                        need(pe, s_fl, n + 3)
                        mm(ps_x[:, 0:128], xt[:, k, 0:128], bas[:, 0, :], start=True, stop=False)
                        mm(ps_x[:, 0:128], xt[:, k, 0:128], bas[:, 1, :], start=False, stop=False)
                        mm(ps_x[:, 0:128], xt[:, k, 128:256], bas[:, 0, :], start=False, stop=True).then_inc(s_fp, 1)
                    if live(i, 0, edge):
                        conv(2)
                    if live(i, 2, edge):
                        k = i % 2
                        if i == -2:
                            pe.wait_ge(s_cw, 2 * B * (l + 1))
                        need(pe, s_fh, n + 3)
                        need(pe, s_fl, n + 3)
                        need(pe, s_y, n + 2)
                        mm(ps_z[:, 0:GC], fh[:, k, :], fw[l][:, 0, :], start=True, stop=False)
                        mm(ps_z[:, 0:GC], fh[:, k, :], fw[l][:, 1, :], start=False, stop=False)
                        mm(ps_z[:, 0:GC], fl[:, k, :], fw[l][:, 0, :], start=False, stop=True).then_inc(s_z, 1)
                    if live(i, 0, edge):
                        conv(3)
                        k = i % 2
                        need(pe, s_yh, n + 1)
                        mm(s[:, 0:GC], bas[:, 2, :], yh[:, k, :], start=False, stop=False)
                        mm(s[:, 0:GC], bas[:, 3, :], yh[:, k, :], start=False, stop=False)
                        need(pe, s_yl, n + 1)
                        mm(s[:, 0:GC], bas[:, 2, :], yl[:, k, :], start=False, stop=True).then_inc(s_s, 1)
                    if live(i, -1, edge):
                        k = (i - 1) % 2
                        need(pe, s_f, n)
                        need(pe, s_ft, n - 1)
                        for b in range(B):
                            t = nc.tensor.transpose(ps_ft[0:HID, b * 128:(b + 1) * 128],
                                                    f[:, k, HID * b:HID * (b + 1)], id32[:, :])
                        t.then_inc(s_ftp, 1)
                    if live(i, -2, edge):
                        k = i % 2
                        need(pe, s_ft, n - 1)
                        need(pe, s_res, n - 2)
                        for b in range(B):
                            o = mm(ps_o[C * b:C * b + C, 0:128], wo[l][:, :], ft[:, k, b * 128:(b + 1) * 128],
                                   start=True, stop=True)
                        o.then_inc(s_o, 1)

                schedule(pe, step)

        @block.scalar
        def _(act):
            def arrange(l):
                act.wait_ge(s_scaled, l + 1)
                need(act, s_cw, 2 * B * l)
                need(act, s_ready, TAPS * l)
                nc.scalar.activation(wh[:, :], win[l][:, :], ACT.Copy).then_inc(s_wh, 1)
                act.wait_ge(s_v32, l + 1)
                nc.scalar.activation(vh[:, :, :].rearrange("p t o -> p (t o)"), wdw[l][:, :], ACT.Copy).then_inc(s_vh, 1)
                act.wait_ge(s_wl, l + 1)
                act.wait_ge(s_wh, l + 1)
                for part, src in enumerate((wh, wl)):
                    for b in range(B):
                        rows = slice(C * b, C * b + C)
                        nc.scalar.activation(fw[l][rows, part, HID * b:HID * b + HID],
                                             src[rows, HID:2 * HID], ACT.Copy).then_inc(s_cw, 1)

            load_weights(act, 1)
            arrange(0)
            for l in range(LAYERS):
                base = l * POS
                if l == 0:
                    act.wait_ge(s_zero, 4)

                def hi_part(s, it, dy, l=l):
                    act.wait_ge(s_xn, l * STRIPS + s + 2 * it + 1)
                    if dy == HI_ORDER[0]:
                        need(act, s_s, l * POS + (s - 2 + 2 * it) * TPS + 1 if l or s > 1 else 0)
                        need(act, s_xtp, l * POS + (s - 1 + 2 * it) * TPS)
                    nc.scalar.activation(
                        parts[s % 2][:, 0, 1 + dy, TH:TH + SW].rearrange("p (w r) -> p w r", r=TH),
                        xn[:, 1 + dy:1 + dy + TH, :].rearrange("p r w -> p w r"),
                        ACT.Copy).then_inc(s_xh, 1)

                for dy in HI_ORDER:
                    hi_part(0, 0, dy)

                def step(i, it, edge, l=l, base=base):
                    n = base + i + UNROLL * it
                    if live(i, 4, edge):
                        need(act, s_xtp, n + 5)
                        need(act, s_fp, n + 3)
                        nc.scalar.activation(xt[:, i % 2, :], ps_xt[:, 0:256], ACT.Copy).then_inc(s_xt, 1)
                    if live(i, 3, edge):
                        need(act, s_fp, n + 4)
                        need(act, s_z, n + 2)
                        nc.scalar.activation(fh[:, (i + 3) % 2, :], ps_x[:, 0:128], ACT.Copy,
                                             scale=1.0 / BS).then_inc(s_fh, 1)
                    if live(i, 0, edge):
                        need(act, s_gate, n + 1)
                        need(act, s_f, n - 1)
                        nc.scalar.activation(g[:, i % 2, :], ps_g[:, 0:GC], ACT.Gelu,
                                             scale=gsc[l][:, 0:1]).then_inc(s_gelu, 1)
                    if live(i, 2, edge):
                        need(act, s_y, n + 3)
                        need(act, s_s, n + 1)
                        nc.scalar.activation(yh[:, i % 2, :], y32[:, i % 2, :], ACT.Copy).then_inc(s_yh, 1)
                    if live(i, -1, edge):
                        need(act, s_ftp, n)
                        need(act, s_o, n - 2)
                        nc.scalar.activation(ft[:, (i - 1) % 2, :], ps_ft[0:HID, 0:B * 128],
                                             ACT.Copy).then_inc(s_ft, 1)
                    s, k = staged(i)
                    if 0 <= k < 3 and (not edge or s < STRIPS):
                        hi_part(s, it, HI_ORDER[k])
                if l == 0:
                    arrange(1)
                schedule(act, step)

        @block.gpsimd
        def _(pool):
            nc.gpsimd.memset(power[:, :], -0.5).then_inc(s_power, 1)
            pool.wait_ge(s_power, 1)
            pool.wait_ge(s_amax, 1)
            nc.gpsimd.partition_all_reduce(amaxr[:, :, :].rearrange("p a b -> p (a b)"), amax[:, :, :].rearrange("p a b -> p (a b)"),
                                           128, RMAX).then_inc(s_all, 1)
            for l in range(LAYERS):
                base = l * POS
                pool.wait_ge(s_var, l + 1)
                nc.gpsimd.tensor_tensor(nr[:, 0:1], ve[:, :], power[:, :], ALU.pow).then_inc(s_root, 1)
                load_stacks(pool, l, 0, SHARED, s_first)

                def step(i, it, edge, base=base):
                    n = base + i + UNROLL * it
                    if live(i, 2, edge):
                        k = i % 2
                        need(pool, s_yh, n + 3)
                        need(pool, s_s, n + 1)
                        nc.gpsimd.tensor_tensor(yl[:, k, :], y32[:, k, :], yh[:, k, :],
                                                ALU.subtract).then_inc(s_yl, 1)
                schedule(pool, step)

        @block.vector
        def _(dve):
            links = [0]
            v = nc.vector

            def link(ins):
                links[0] += 1
                ins.then_inc(s_chain, 1)
                dve.wait_ge(s_chain, links[0])

            for i in range(2):
                v.memset(parts[i][:, :, :, 0:TH], 0.0).then_inc(s_zero, 1)
                v.memset(parts[i][:, :, :, SC - TH:SC], 0.0).then_inc(s_zero, 1)
                v.memset(stack[i][2 * C:3 * C, GATE, :, :], 0.0)
            v.memset(x[:, 0, :], 0.0)
            v.memset(x[:, H + 1, :], 0.0)

            def maxima():
                for l in range(LAYERS):
                    dve.wait_ge(s_w[l], 16 * (B + 2))
                    for k, raw in enumerate((win[l], wdw[l], fft[l])):
                        rows = raw.shape[0]
                        last = v.tensor_reduce(amax[0:rows, k, l:l + 1], raw[:, :], AX.X, ALU.max,
                                               apply_absolute_value=True)
                last.then_inc(s_amax, 1)

            def scales():
                dve.wait_ge(s_all, 1)
                v.tensor_scalar(tops[:, 0, :], amaxr[:, 0, :], 1e-30, None, ALU.max)
                link(v.scalar_tensor_tensor(tops[:, 1, :], amaxr[:, 1, :], 1e-30, amaxr[:, 2, :], ALU.max, ALU.max))
                link(v.tensor_scalar(p2[:, :, :].bitcast(I32), tops[:, :, :].bitcast(I32), 0x7F800000, None,
                                     ALU.bitwise_and))
                link(v.reciprocal(ip2[:, :, :], p2[:, :, :]))
                for l in range(LAYERS):
                    v.tensor_scalar(gsc[l][:, :], p2[:, 0, l:l + 1], 1.0 / SS, None, ALU.mult)
                    v.tensor_scalar(osc[l][:, :], p2[:, 0, l:l + 1], p2[:, 1, l:l + 1], 1.0 / SS, ALU.mult, ALU.mult)

            def prepare(l):
                v.tensor_scalar(win[l][:, :], win[l][:, :], ip2[:, 0, l:l + 1], WS, ALU.mult,
                                ALU.mult).then_inc(s_scaled, 1)
                dve.wait_ge(s_scaled, l + 1)
                taps = wdw[l][:, :].rearrange("p (t o) -> p t o", t=9)
                v.scalar_tensor_tensor(taps, taps, ip2[:, 1, l:l + 1], win[l][:, None, 0:HID].broadcast_to([128, 9, HID]),
                                       ALU.mult, ALU.mult).then_inc(s_v32, 1)
                dve.wait_ge(s_fold, l + 1)
                v.tensor_scalar(weff[l][:, :], (ps_x, ps_ft)[l][:, 0:HID], ip2[:, 1, l:l + 1], 1.0 / BS, ALU.mult,
                                ALU.mult)
                dve.wait_ge(s_wh, l + 1)
                need(dve, s_cw, 2 * B * l)
                v.tensor_tensor(wl[:, :], win[l][:, :], wh[:, :], ALU.subtract).then_inc(s_wl, 1)
                dve.wait_ge(s_wl, l + 1)
                dve.wait_ge(s_vh, l + 1)
                dve.wait_ge(s_v32, l + 1)
                link(v.tensor_tensor(vl[:, :, :], taps, vh[:, :, :], ALU.subtract))
                for m0, (part, last) in ((0, (vh, 0)), (3, (vl, 1))):
                    for k, (src, dy) in enumerate(((part, -1), (part, 0), (part, 1), (vh, last))):
                        rows = slice(C * k, C * k + C)
                        v.tensor_copy(cw[l][rows, m0:m0 + 3, :],
                                      src[rows, 3 * dy + 3:3 * dy + 6, :]).then_inc(s_ready, 1)
                for k in range(3):
                    rows = slice(C * k, C * k + C)
                    v.tensor_copy(cw[l][rows, 6, :], vh[rows, k, :]).then_inc(s_ready, 1)
                for k, src in ((0, wh), (1, wl), (3, wh)):
                    rows = slice(C * k, C * k + C)
                    v.tensor_copy(gw[l][rows, :], src[rows, 2 * HID:3 * HID]).then_inc(s_ready, 1)

            for l in range(LAYERS):
                v.memset(gw[l][:, :], 0.0)
                v.memset(fw[l][:, :, :], 0.0)
            link(v.memset(amax[:, :, :], 0.0))

            def strip_stats(s, it=0):
                for h in range(2):
                    row = 1 + TH * s + TH // 2 * h + 2 * TH * it
                    last = v.bn_stats(st[:, bass.ds(2 * s + h + 4 * it, 1), :].rearrange("p a b -> p (a b)"),
                                      x[:, bass.ds(row, TH // 2), :].rearrange("p r w -> p (r w)"))
                return last

            maxima()
            for s in range(STRIPS):
                if s == STRIPS // 4:
                    scales()
                    prepare(0)
                dve.wait_ge(s_x[s], 16)
                last = strip_stats(s)
            link(last)
            for l in range(LAYERS):
                base = l * POS
                link(v.bn_aggr(mv[:, :], st[:, :, :].rearrange("p a b -> p (a b)")))
                v.tensor_scalar(ve[:, :], mv[:, 1:2], EPS, None, ALU.add).then_inc(s_var, 1)
                dve.wait_ge(s_root, l + 1)
                link(v.tensor_scalar(nr[:, 1:2], nr[:, 0:1], nr[:, 0:1], ve[:, 0:1], ALU.mult, ALU.mult))
                link(v.tensor_scalar(nr[:, 2:3], nr[:, 1:2], -0.5, 1.5, ALU.mult, ALU.add))
                link(v.tensor_scalar(rstd[:, :], nr[:, 2:3], nr[:, 0:1], XS, ALU.mult, ALU.mult))

                for row in (0, H + 1):
                    last = v.tensor_scalar(x[:, row, :], x[:, row, :], 0.0, mv[:, 0:1], ALU.mult, ALU.add)
                link(last)

                def norm(s, it, l=l):
                    need(dve, s_xl, 3 * (l * STRIPS + s - 1 + 2 * it))
                    v.tensor_scalar(xn[:, :, :], x[:, bass.ds(TH * s + 2 * TH * it, TH + 2), :], mv[:, 0:1],
                                    rstd[:, 0:1], ALU.subtract, ALU.mult).then_inc(s_xn, 1)

                def lo_part(s, it, dy, l=l):
                    dve.wait_ge(s_xh, 3 * (l * STRIPS + s + 2 * it) + HI_ORDER.index(dy) + 1)
                    part = parts[s % 2][:, :, 1 + dy, TH:TH + SW].rearrange("p a (w r) -> p a w r", r=TH)
                    v.tensor_tensor(part[:, 1], xn[:, 1 + dy:1 + dy + TH, :].rearrange("p r w -> p w r"),
                                    part[:, 0], ALU.subtract).then_inc(s_xl, 1)

                def copy_groups(s, it, loads, l=l):
                    if s == 0:
                        need(dve, s_s, l * POS - TPS)
                    dve.wait_ge(s_xh, 3 * (l * STRIPS + s + 1 + 2 * it))
                    dve.wait_ge(s_xl, 3 * (l * STRIPS + s + 1 + 2 * it))
                    for load in loads:
                        dst, src = group_ap(s, load)
                        v.tensor_copy(dst, src).then_inc(s_copy, 1)

                norm(0, 0)
                for dy in LO_ORDER:
                    lo_part(0, 0, dy)
                copy_groups(0, 0, BY_COPY)
                if l == 0:
                    prepare(1)

                def step(i, it, edge, l=l, base=base):
                    n = base + i + UNROLL * it
                    if live(i, -1, edge):
                        k = (i - 1) % 2
                        need(dve, s_s, n)
                        need(dve, s_gelu, n)
                        if l + 1 < LAYERS and i % TPS == 2:
                            need(dve, s_res, n - 2)
                        need(dve, s_ftp, n - 2)
                        v.tensor_tensor(f[:, k, :], ps_s[k][:, 0:GC], g[:, k, :], ALU.mult).then_inc(s_f, 1)
                        if l + 1 < LAYERS and i % TPS == 2 and i > TPS:
                            strip_stats(i // TPS - 1, it)
                    if live(i, 3, edge):
                        k = (i + 3) % 2
                        need(dve, s_fh, n + 4)
                        need(dve, s_z, n + 2)
                        v.scalar_tensor_tensor(fl[:, k, :], ps_x[:, 0:128], 1.0 / BS, fh[:, k, :],
                                               ALU.mult, ALU.subtract).then_inc(s_fl, 1)
                    if live(i, 2, edge):
                        k = i % 2
                        need(dve, s_z, n + 3)
                        need(dve, s_yl, n + 1)
                        v.tensor_tensor(y32[:, k, :].rearrange("p (b o) -> p b o", b=B),
                                        ps_z[:, 0:GC].rearrange("p (b o) -> p b o", b=B),
                                        weff[l][:, None, :].broadcast_to([128, B, HID]),
                                        ALU.mult).then_inc(s_y, 1)
                    if live(i, -2, edge):
                        q = i - 2
                        need(dve, s_o, n - 1)
                        xv = x[:, bass.ds(1 + TH * (q // TPS) + 2 * TH * it, TH),
                               TW * (q % TPS):TW * (q % TPS) + TW].rearrange("p r w -> p w r")
                        v.scalar_tensor_tensor(xv, ps_o[:, 0:128].rearrange("p (w r) -> p w r", r=TH),
                                               osc[l][:, 0:1], xv, ALU.mult, ALU.add).then_inc(s_res, 1)
                    s, k = staged(i)
                    if k >= 0 and (not edge or s < STRIPS):
                        if k == 0:
                            norm(s, it)
                        else:
                            lo_part(s, it, LO_ORDER[k - 1])
                    s, k = i // TPS + 1, i % TPS - 1
                    if 0 <= k < COPY_STEPS and s > 0 and (not edge or s < STRIPS):
                        copy_groups(s, it, BY_COPY[k::COPY_STEPS])
                schedule(dve, step)
                if l + 1 < LAYERS:
                    dve.wait_ge(s_res, base + POS)
                    link(strip_stats(STRIPS - 1))


def fourier():
    yy, xx = np.meshgrid(np.arange(P), np.arange(P), indexing="ij")
    comps, sources, seen = [], [], set()
    for kh in range(P):
        for kw in range(P // 2 + 1):
            if (kh, kw) in seen:
                continue
            mirror = ((-kh) % P, (-kw) % P)
            seen |= {(kh, kw), mirror}
            theta = 2 * np.pi * (kh * yy + kw * xx) / P
            src = [(kh, kw), mirror] if kw in (0, P // 2) else [(kh, kw)]
            if mirror == (kh, kw):
                comps.append(np.cos(theta) / P)
                sources.append(src[:1])
            else:
                for wave in (np.cos(theta), np.sin(theta)):
                    comps.append(wave * np.sqrt(2) / P)
                    sources.append(src)
    assert len(comps) == P * P
    return np.stack([c.reshape(-1) for c in comps], 1), sources


def constants():
    basis, sources = fourier()
    full = np.zeros((PIX, PIX))
    for pix in range(PIX):
        c, r = divmod(pix, TH)
        full[pix, (c // P) * P * P:(c // P + 1) * P * P] = basis[r * P + c % P]
    full *= BS
    packed = np.zeros((128, 4, 128), np.float16)
    for k, m in enumerate((full, full.T)):
        packed[:, 2 * k] = m.astype(np.float16)
        packed[:, 2 * k + 1] = (m - packed[:, 2 * k].astype(np.float64)).astype(np.float16)
    fold = np.zeros((P * (P // 2 + 1), 128), np.float32)
    for k, src in enumerate(sources):
        for kh, kw in src:
            fold[kh * (P // 2 + 1) + kw, [k, P * P + k]] += 1.0 / len(src)
    return {"basis": packed, "eye16": np.eye(128, dtype=np.float16), "eye32": np.eye(128, dtype=np.float32),
            "fold": fold}


def kernel(**inputs):
    import concourse.bacc as bacc
    from concourse.bass_utils import run_bass_kernel_spmd

    arrays = {"x": np.ascontiguousarray(np.asarray(inputs["x"]).reshape(B * C, H * W))}
    for l in range(LAYERS):
        raw = {k: np.asarray(inputs[f"L{l}_conv_{k}"]) for k in ("W_in", "W_dw", "fft_weight", "W_out")}
        arrays[f"w_in{l}"] = np.ascontiguousarray(raw["W_in"].T)
        arrays[f"w_dw{l}"] = np.ascontiguousarray(raw["W_dw"].reshape(HID, 9).T.reshape(9 * HID))
        arrays[f"w_fft{l}"] = np.ascontiguousarray(raw["fft_weight"].reshape(HID, -1).T)
        arrays[f"w_out{l}"] = np.ascontiguousarray(raw["W_out"].T)
    arrays.update(constants())

    nc = bacc.Bacc("TRN2", target_bir_lowering=False, num_devices=1)
    ap = {k: nc.dram_tensor("in_" + k, a.shape, mybir.dt.from_np(a.dtype), kind="ExternalInput").ap()
          for k, a in arrays.items()}
    y = nc.dram_tensor("out_y", (B * C, H * W), F32, kind="ExternalOutput").ap()
    per_layer = [[ap[f"{k}{l}"] for l in range(LAYERS)] for k in ("w_in", "w_dw", "w_fft", "w_out")]
    build(nc, ap["x"], *per_layer, ap["basis"], ap["eye16"], ap["eye32"], ap["fold"], y)
    got = run_bass_kernel_spmd(nc, [{"in_" + k: a for k, a in arrays.items()}], core_ids=[0])
    return got.results[0]["out_y"].reshape(B, C, H, W)
```

```python
from contextlib import ExitStack

import numpy as np

import concourse.bass as bass
import concourse.mybir as mybir

F32 = mybir.dt.float32
F16 = mybir.dt.float16
I32 = mybir.dt.int32
ALU = mybir.AluOpType
ACT = mybir.ActivationFunctionType
AX = mybir.AxisListType
RMAX = bass.bass_isa.ReduceOp.max

LAYERS = 2
B, C, H, W = 4, 32, 128, 128
HID = 85
P = 8
TH, TW = 8, 16
PIX = TH * TW
STRIPS = H // TH
TPS = W // TW
POS = STRIPS * TPS
SC = TH * (W + 2)
SW = TH * W
GC = B * HID
XS = 16.0
WS = 32.0
BS = 256.0
US = 1 / 128
SS = XS * WS
UNROLL = 2 * TPS
EPS = 1e-5
MAIN, ALT, GATE, THIRD = range(4)
STACKS = 4
HI_ORDER = (0, -1, 1)
LO_ORDER = (0, -1, 1)
PASSES = [(MAIN, -1), (MAIN, 0), (MAIN, 1), (ALT, -1), (ALT, 0), (ALT, 1), (THIRD, -1)]
NPASS = len(PASSES)
PROJECTIONS = 3
TAPS = 11
PLACED = PROJECTIONS + TAPS
GROUPS = [(1, slice(MAIN, GATE + 1), 0, 0, 0), (0, slice(MAIN, ALT + 1), 0, -1, 0), (2, slice(MAIN, ALT + 1), 0, 1, 0),
          (0, slice(GATE, GATE + 1), 0, 0, 0), (3, slice(MAIN, GATE + 1, 2), 1, 0, 0),
          (0, slice(THIRD, THIRD + 1), 1, -1, 0), (1, slice(THIRD, THIRD + 1), 1, -1, 1),
          (2, slice(THIRD, THIRD + 1), 1, -1, 2), (3, slice(ALT, ALT + 1), 1, 1, 0)]
LOADS = [[(b, group) for b in range(B)] for group in GROUPS]
PLAIN = LOADS[0] + LOADS[3] + LOADS[4]


def parted(loads):
    return [load for load in loads if load in PLAIN], [load for load in loads if load not in PLAIN]


BY_DMA = PLAIN + LOADS[1] + LOADS[2] + LOADS[5] + LOADS[8]
BY_COPY = LOADS[6] + LOADS[7]
FIRST_BY_ACT = LOADS[5]
FIRST_BY_COPY = BY_COPY + LOADS[8]
FIRST_BY_DMA = LOADS[0] + LOADS[3] + LOADS[4] + LOADS[1] + LOADS[2]
FIRST_BY_POOL = FIRST_BY_DMA[2::3] + FIRST_BY_DMA[-1:]
FIRST_BY_SP = [load for load in FIRST_BY_DMA if load not in FIRST_BY_POOL]


def build(nc, x_in, w_raw, w_fft, w_out, basis, eye32, fold, y_out):
    ctx = ExitStack()
    with ctx:
        def sb(name, shape, dt=F32):
            return ctx.enter_context(nc.sbuf_tensor(name, shape, dt))

        def sem(name):
            return ctx.enter_context(nc.semaphore(name))

        x = sb("x", [128, H + 2, W])
        xn = sb("xn", [128, TH + 2, W])
        parts = [sb(f"parts{i}", [128, 2, 3, SC], F16) for i in range(2)]
        stack = [sb(f"stack{i}", [128, STACKS, B, SC], F16) for i in range(2)]
        bas = sb("bas", [128, 4, 128], F16)
        id32 = sb("id32", [128, 128])
        fold_sb = sb("fold_sb", [P * (P // 2 + 1), 128])
        raw = [sb(f"raw{i}", [128, 12 * HID]) for i in range(LAYERS)]
        win = [r[:, 0:3 * HID] for r in raw]
        wdw = [r[:, 3 * HID:] for r in raw]
        fft = [sb(f"fft{i}", [P * (P // 2 + 1), HID]) for i in range(LAYERS)]
        vh = sb("vh", [128, 9, HID], F16)
        vl = sb("vl", [128, 9, HID], F16)
        wh = sb("wh", [128, 3 * HID], F16)
        wl = sb("wl", [128, 3 * HID], F16)
        amax = sb("amax", [128, 3, LAYERS])
        amaxr = sb("amaxr", [128, 3, LAYERS])
        tops = sb("tops", [128, 2, LAYERS])
        p2 = sb("p2", [128, 2, LAYERS])
        ip2 = sb("ip2", [128, 2, LAYERS])
        cw = [sb(f"cw{i}", [128, NPASS, HID], F16) for i in range(LAYERS)]
        pw = [sb(f"pw{i}", [128, 2, HID], F16) for i in range(LAYERS)]
        weff = [sb(f"weff{i}", [128, HID]) for i in range(LAYERS)]
        wo = [sb(f"wo{i}", [HID, C]) for i in range(LAYERS)]
        gsc = [sb(f"gsc{i}", [128, 1]) for i in range(LAYERS)]
        osc = [sb(f"osc{i}", [128, 1]) for i in range(LAYERS)]
        st = sb("st", [128, 2 * STRIPS, 6])
        mv = sb("mv", [128, 2])
        ve = sb("ve", [128, 1])
        power = sb("power", [128, 1])
        nr = sb("nr", [128, 4])
        rstd = sb("rstd", [128, 1])
        uh = sb("uh", [128, 2, GC], F16)
        ul = sb("ul", [128, 2, GC], F16)
        g = sb("g", [128, 2, GC])
        y32 = sb("y32", [128, 2, GC])
        yh = sb("yh", [128, 2, GC], F16)
        yl = sb("yl", [128, 2, GC], F16)
        f = sb("f", [128, 2, GC])
        ft = sb("ft", [HID, 2, B * 128])

        def bank(name):
            return ctx.enter_context(nc.psum_tensor(name, [128, 512], F32))
        ps_s = [bank("ps_s0"), bank("ps_s1")]
        ps_u = [bank("ps_u0"), bank("ps_u1")]
        ps_g, ps_z, ps_ft, ps_o = (bank(n) for n in ("ps_g", "ps_z", "ps_ft", "ps_o"))

        s_const = sem("s_const")
        s_basis = sem("s_basis")
        s_w = [sem(f"s_w{i}") for i in range(LAYERS)]
        s_wo = sem("s_wo")
        s_x = [sem(f"s_x{i}") for i in range(STRIPS)]
        s_zero = sem("s_zero")
        s_idle = sem("s_idle")
        s_amax = sem("s_amax")
        s_all = sem("s_all")
        s_fold = sem("s_fold")
        s_weff = sem("s_weff")
        s_chain = sem("s_chain")
        s_ready = sem("s_ready")
        s_scaled = sem("s_scaled")
        s_merged = sem("s_merged")
        s_wh = sem("s_wh")
        s_wl = sem("s_wl")
        s_vh = sem("s_vh")
        s_vl = sem("s_vl")
        s_var = sem("s_var")
        s_root = sem("s_root")
        s_power = sem("s_power")
        s_xn = sem("s_xn")
        s_xh = sem("s_xh")
        s_xl = sem("s_xl")
        s_stk = [[sem(f"s_stk_{kind}{i}") for kind in ("gate", "conv")] for i in range(2)]
        s_first = [sem(f"s_first_{kind}") for kind in ("gate", "conv")]
        s_acopy = sem("s_acopy")
        s_copy = sem("s_copy")
        s_u = sem("s_u")
        s_uh = sem("s_uh")
        s_ul = sem("s_ul")
        s_z = sem("s_z")
        s_y = sem("s_y")
        s_yh = sem("s_yh")
        s_yl = sem("s_yl")
        s_gate = sem("s_gate")
        s_gelu = sem("s_gelu")
        s_s = sem("s_s")
        s_f = sem("s_f")
        s_ftp = sem("s_ftp")
        s_ft = sem("s_ft")
        s_o = sem("s_o")
        s_res = sem("s_res")
        s_out = sem("s_out")

        block = ctx.enter_context(nc.Block())

        def need(eng, semaphore, value):
            if not isinstance(value, int) or value > 0:
                eng.wait_ge(semaphore, value)

        LEAD = 3
        FIRST = 4
        ITERS = (POS - LEAD - FIRST) // UNROLL
        TAIL = FIRST + ITERS * UNROLL

        def schedule(eng, step):
            for i in range(-LEAD, FIRST):
                step(i, 0, True)
            with eng.Fori(0, ITERS) as it:
                for i in range(FIRST, FIRST + UNROLL):
                    step(i, it, False)
            for i in range(TAIL, POS + 2):
                step(i, 0, True)

        def live(i, offset, edge):
            return not edge or 0 <= i + offset < POS

        def staged(i):
            if i < FIRST:
                return 1, i + 1 if i >= -1 else None
            s, part = (i // TPS + 1, 4) if i % TPS == 0 else (i // TPS + 2, i % TPS - 4)
            return s, part if part >= 0 and s < STRIPS else None

        def copied(i):
            halves = (3, 5)
            s, k = i // TPS + 1, i % TPS
            return s, halves.index(k) if k in halves and s < STRIPS and i > 0 else None

        def group_ap(s, load):
            b, (k, kinds, part, dy, dx) = load
            dst = stack[s % 2][C * k:C * k + C, kinds, b, 0:SC - TH * dx]
            src = parts[s % 2][C * b:C * b + C, part, 1 + dy, TH * dx:SC]
            return dst, src[:, None, :].broadcast_to([C, len(range(*kinds.indices(STACKS))), SC - TH * dx])

        def load_stacks(eng, l, s, loads, loaded):
            need(eng, s_s, l * POS + (s - 1) * TPS)
            waited = None
            for load in loads:
                part, dy = load[1][2:4]
                if (part, dy) != waited:
                    waited = (part, dy)
                    eng.wait_ge((s_xh, s_xl)[part], 3 * (l * STRIPS + s) + (HI_ORDER, LO_ORDER)[part].index(dy) + 1)
                dst, src = group_ap(s, load)
                eng.dma_start(dst, src).then_inc(loaded[load not in PLAIN], 16)

        def store(sp, s):
            sp.wait_ge(s_res, (LAYERS - 1) * POS + (s + 1) * TPS)
            sp.dma_start(y_out[:, s * SW:(s + 1) * SW], x[:, 1 + TH * s:1 + TH * s + TH, :].rearrange("p r w -> p (r w)")).then_inc(s_out, 16)

        @block.sync
        def _(sp):
            def load_weights(l):
                sp.dma_start(raw[l][:, :], w_raw[l]).then_inc(s_w[l], 16)
                sp.dma_start(fft[l][:, :], w_fft[l]).then_inc(s_w[l], 16)

            for s in range(STRIPS):
                if s == 1:
                    load_weights(0)
                    load_weights(1)
                    sp.dma_start(fold_sb[:, :], fold).then_inc(s_basis, 16)
                sp.dma_start(x[:, 1 + TH * s:1 + TH * s + TH, :].rearrange("p r w -> p (r w)"), x_in[:, s * SW:(s + 1) * SW]).then_inc(s_x[s], 16)
            sp.dma_start(bas[:, :, :], basis).then_inc(s_const, 16)
            sp.dma_start(id32[:, :], eye32).then_inc(s_const, 16)
            for l in range(LAYERS):
                sp.dma_start(wo[l][:, :], w_out[l]).then_inc(s_wo, 16)
            for l in range(LAYERS):
                for s in range(STRIPS):
                    load_stacks(sp, l, s, BY_DMA if s else FIRST_BY_SP, s_stk[s % 2])
                    if l == LAYERS - 1 and s >= 2:
                        store(sp, s - 2)
            for s in (STRIPS - 2, STRIPS - 1):
                store(sp, s)
            sp.wait_ge(s_out, 16 * STRIPS)

        @block.tensor
        def _(pe):
            mm = nc.tensor.matmul
            pe.wait_ge(s_basis, 16)
            for l in range(LAYERS):
                pe.wait_ge(s_w[l], 32)
                mm(ps_u[l][:, 0:HID], fold_sb[:, :], fft[l][:, :], start=True, stop=True).then_inc(s_fold, 1)
            pe.wait_ge(s_const, 32)
            for l in range(LAYERS):
                base = l * POS

                def step(i, it, edge, l=l, base=base):
                    n = base + i + UNROLL * it

                    s = ps_s[i % 2]

                    def pixels(kind, i, b, dx, rows=128):
                        col = TH * (1 + TW * (i % TPS) + dx)
                        return stack[(i // TPS) % 2][0:rows, kind, b, col:col + PIX]

                    def conv(b):
                        for m, (kind, dx) in enumerate(PASSES):
                            rows = 3 * C if kind == THIRD else 128
                            mm(s[:, HID * b:HID * (b + 1)], pixels(kind, i, b, dx, rows), cw[l][0:rows, m, :],
                               start=(b == 0 and m == 0), stop=False)

                    def project(bank, which, i, images):
                        for b in images:
                            t = mm(bank[:, HID * b:HID * (b + 1)], pixels(GATE, i, b, 0), pw[l][:, which, :],
                                   start=(b == 0), stop=(b == B - 1))
                        return t

                    def stacks_loaded(s, conv):
                        strips = l * (STRIPS // 2) + s // 2 + 1 + it
                        usual, first = len(parted(BY_DMA)[conv]), len(parted(FIRST_BY_SP)[conv])
                        less = 0 if s % 2 else (l + 1) * (usual - first)
                        pe.wait_ge(s_stk[s % 2][conv], strips * (16 * usual) - 16 * less)
                        if s == 0:
                            pe.wait_ge(s_first[conv], (l + 1) * 16 * len(parted(FIRST_BY_POOL)[conv]))

                    if live(i, 0, edge):
                        need(pe, s_f, n - 1)
                        if i % TPS == 0:
                            stacks_loaded(i // TPS, 1)
                            more = (l + 1) * (len(FIRST_BY_COPY) - len(BY_COPY))
                            pe.wait_ge(s_copy, (l * STRIPS + i // TPS + 1 + 2 * it) * len(BY_COPY) + more)
                        if i == 0:
                            pe.wait_ge(s_acopy, (l + 1) * len(FIRST_BY_ACT))
                        if i == 0:
                            pe.wait_ge(s_ready, PLACED * (l + 1))
                            pe.wait_ge(s_wo, 16 * LAYERS)
                        conv(0)
                    if live(i, -2, edge):
                        k = i % 2
                        need(pe, s_f, n - 1)
                        need(pe, s_ft, n - 2)
                        for b in range(B):
                            t = nc.tensor.transpose(ps_ft[0:HID, b * 128:(b + 1) * 128],
                                                    f[:, k, HID * b:HID * (b + 1)], id32[:, :])
                        t.then_inc(s_ftp, 1)
                    if live(i, 0, edge):
                        need(pe, s_gelu, n)
                        project(ps_g, 1, i, range(B // 2))
                        conv(1)
                    if live(i, 3, edge):
                        if (i + 3) % TPS == 0:
                            stacks_loaded((i + 3) // TPS, 0)
                        if i == -3:
                            pe.wait_ge(s_idle, 2)
                            pe.wait_ge(s_ready, PLACED * l + PROJECTIONS)
                            pe.wait_ge(s_weff, LAYERS)
                        need(pe, s_uh, n + 2)
                        need(pe, s_ul, n + 2)
                        project(ps_u[(i + 3) % 2], 0, i + 3, range(B)).then_inc(s_u, 1)
                    if live(i, 0, edge):
                        project(ps_g, 1, i, range(B // 2, B)).then_inc(s_gate, 1)
                        conv(2)
                    if live(i, 2, edge):
                        k = i % 2
                        need(pe, s_uh, n + 3)
                        need(pe, s_y, n + 2)
                        mm(ps_z[:, 0:GC], bas[:, 0, :], uh[:, k, :], start=True, stop=False)
                        mm(ps_z[:, 0:GC], bas[:, 1, :], uh[:, k, :], start=False, stop=False)
                        need(pe, s_ul, n + 3)
                        mm(ps_z[:, 0:GC], bas[:, 0, :], ul[:, k, :], start=False, stop=True).then_inc(s_z, 1)
                    if live(i, 0, edge):
                        conv(3)
                        k = i % 2
                        need(pe, s_yh, n + 1)
                        mm(s[:, 0:GC], bas[:, 2, :], yh[:, k, :], start=False, stop=False)
                        mm(s[:, 0:GC], bas[:, 3, :], yh[:, k, :], start=False, stop=False)
                        need(pe, s_yl, n + 1)
                        mm(s[:, 0:GC], bas[:, 2, :], yl[:, k, :], start=False, stop=True).then_inc(s_s, 1)
                    if live(i, -2, edge):
                        k = i % 2
                        need(pe, s_ft, n - 1)
                        need(pe, s_res, n - 2)
                        for b in range(B):
                            o = mm(ps_o[C * b:C * b + C, 0:128], wo[l][:, :], ft[:, k, b * 128:(b + 1) * 128],
                                   start=True, stop=True)
                        o.then_inc(s_o, 1)

                schedule(pe, step)

        @block.scalar
        def _(act):
            def arrange(l):
                def hi_of_projection():
                    act.wait_ge(s_scaled, l + 1)
                    need(act, s_ready, PLACED * l)
                    need(act, s_wl, l)
                    nc.scalar.activation(wh[:, :], win[l], ACT.Copy).then_inc(s_wh, 1)

                def hi_of_taps():
                    act.wait_ge(s_merged, l + 1)
                    need(act, s_vl, l)
                    nc.scalar.activation(vh[:, :, :].rearrange("p t o -> p (t o)"), wdw[l], ACT.Copy).then_inc(s_vh, 1)

                def place(semaphore, count, copies):
                    act.wait_ge(s_wh, l + 1)
                    act.wait_ge(s_vh, l + 1)
                    act.wait_ge(semaphore, count)
                    for dst, src in copies:
                        nc.scalar.activation(dst, src, ACT.Copy).then_inc(s_ready, 1)

                def rows(group):
                    return slice(C * group, C * group + C)

                of_projections = [(pw[l][rows(k), :, :], src[rows(k), HID:3 * HID].rearrange("p (a o) -> p a o", a=2))
                                  for k, src in ((0, wh), (1, wl), (3, wh))]
                of_taps = [(cw[l][rows(k), m:m + 3, :], src[rows(k), 3 * dy + 3:3 * dy + 6, :])
                           for m, sources in ((0, ((vh, -1), (vh, 0), (vh, 1), (vh, 0))),
                                              (3, ((vl, -1), (vl, 0), (vl, 1), (vh, 1))))
                           for k, (src, dy) in enumerate(sources)]
                of_taps += [(cw[l][rows(k), 6, :], vh[rows(k), k, :]) for k in range(3)]
                assert (len(of_projections), len(of_taps)) == (PROJECTIONS, TAPS)
                return [hi_of_projection, hi_of_taps,
                        lambda: place(s_wl, l + 1, of_projections),
                        lambda: place(s_vl, l + 1, of_taps[:TAPS // 3]),
                        lambda: place(s_vl, l + 1, of_taps[TAPS // 3:2 * TAPS // 3]),
                        lambda: place(s_vl, l + 1, of_taps[2 * TAPS // 3:])]

            act.wait_ge(s_zero, 6)
            for piece in arrange(0):
                piece()
            for l in range(LAYERS):
                base = l * POS
                pieces = arrange(1) if l == 0 else []

                def hi_part(s, it, dy, l=l):
                    act.wait_ge(s_xn, l * STRIPS + s + 2 * it + 1)
                    if dy == HI_ORDER[0]:
                        need(act, s_s, l * POS + (s - 2 + 2 * it) * TPS + 1 if l or s > 1 else 0)
                    nc.scalar.activation(
                        parts[s % 2][:, 0, 1 + dy, TH:TH + SW].rearrange("p (w r) -> p w r", r=TH),
                        xn[:, 1 + dy:1 + dy + TH, :].rearrange("p r w -> p w r"),
                        ACT.Copy).then_inc(s_xh, 1)

                for dy in HI_ORDER:
                    hi_part(0, 0, dy)

                need(act, s_s, l * POS - TPS)
                act.wait_ge(s_xl, 3 * l * STRIPS + LO_ORDER.index(-1) + 1)
                for load in FIRST_BY_ACT:
                    dst, src = group_ap(0, load)
                    nc.scalar.activation(dst, src, ACT.Copy).then_inc(s_acopy, 1)

                def step(i, it, edge, l=l, base=base, pieces=pieces):
                    n = base + i + UNROLL * it
                    if live(i, -2, edge):
                        need(act, s_ftp, n - 1)
                        need(act, s_o, n - 3)
                        nc.scalar.activation(ft[:, i % 2, :], ps_ft[0:HID, 0:B * 128], ACT.Copy).then_inc(s_ft, 1)
                    if live(i, 3, edge):
                        k = (i + 3) % 2
                        need(act, s_u, n + 4)
                        need(act, s_z, n + 2)
                        nc.scalar.activation(uh[:, k, :], ps_u[k][:, 0:GC], ACT.Copy, scale=US).then_inc(s_uh, 1)
                    if live(i, 0, edge):
                        need(act, s_gate, n + 1)
                        need(act, s_f, n - 1)
                        nc.scalar.activation(g[:, i % 2, :], ps_g[:, 0:GC], ACT.Gelu,
                                             scale=gsc[l][:, 0:1]).then_inc(s_gelu, 1)
                    if live(i, 2, edge):
                        need(act, s_y, n + 3)
                        need(act, s_s, n + 1)
                        nc.scalar.activation(yh[:, i % 2, :], y32[:, i % 2, :], ACT.Copy).then_inc(s_yh, 1)
                    s, part = staged(i)
                    if part in (1, 2, 3):
                        hi_part(s, it, HI_ORDER[part - 1])
                    if 0 < i - TAIL <= len(pieces):
                        pieces[i - TAIL - 1]()
                schedule(act, step)

        @block.gpsimd
        def _(pool):
            nc.gpsimd.memset(power[:, :], -0.5).then_inc(s_power, 1)
            pool.wait_ge(s_power, 1)
            for i in range(2):
                nc.gpsimd.memset(stack[i][2 * C:3 * C, GATE, :, :], 0.0).then_inc(s_idle, 1)
                pool.wait_ge(s_idle, i + 1)
            pool.wait_ge(s_amax, 1)
            nc.gpsimd.partition_all_reduce(amaxr[:, :, :].rearrange("p a b -> p (a b)"), amax[:, :, :].rearrange("p a b -> p (a b)"),
                                           128, RMAX).then_inc(s_all, 1)
            for l in range(LAYERS):
                base = l * POS
                pool.wait_ge(s_var, l + 1)
                nc.gpsimd.tensor_tensor(nr[:, 0:1], ve[:, :], power[:, :], ALU.pow).then_inc(s_root, 1)
                load_stacks(pool, l, 0, FIRST_BY_POOL, s_first)

                def step(i, it, edge, base=base):
                    n = base + i + UNROLL * it
                    if live(i, 2, edge):
                        k = i % 2
                        need(pool, s_yh, n + 3)
                        need(pool, s_s, n + 1)
                        nc.gpsimd.tensor_tensor(yl[:, k, :], y32[:, k, :], yh[:, k, :],
                                                ALU.subtract).then_inc(s_yl, 1)
                schedule(pool, step)

        @block.vector
        def _(dve):
            links = [0]
            v = nc.vector

            def link(ins):
                links[0] += 1
                ins.then_inc(s_chain, 1)
                dve.wait_ge(s_chain, links[0])

            def maxima():
                for l in range(LAYERS):
                    dve.wait_ge(s_w[l], 32)
                    for k, (rows, w) in enumerate(((128, win[l]), (128, wdw[l]), (P * (P // 2 + 1), fft[l][:, :]))):
                        last = v.tensor_reduce(amax[0:rows, k, l:l + 1], w, AX.X, ALU.max,
                                               apply_absolute_value=True)
                last.then_inc(s_amax, 1)

            def scales():
                dve.wait_ge(s_all, 1)
                v.tensor_scalar(tops[:, 0, :], amaxr[:, 0, :], 1e-30, None, ALU.max)
                link(v.scalar_tensor_tensor(tops[:, 1, :], amaxr[:, 1, :], 1e-30, amaxr[:, 2, :], ALU.max, ALU.max))
                link(v.tensor_scalar(p2[:, :, :].bitcast(I32), tops[:, :, :].bitcast(I32), 0x7F800000, None,
                                     ALU.bitwise_and))
                link(v.reciprocal(ip2[:, :, :], p2[:, :, :]))
                for l in range(LAYERS):
                    v.tensor_scalar(gsc[l][:, :], p2[:, 0, l:l + 1], 1.0 / SS, None, ALU.mult)
                    v.tensor_scalar(osc[l][:, :], p2[:, 0, l:l + 1], p2[:, 1, l:l + 1], 1.0 / SS, ALU.mult, ALU.mult)

            def prepare(l):
                taps = wdw[l].rearrange("p (t o) -> p t o", t=9)

                def scale():
                    v.tensor_scalar(win[l], win[l], ip2[:, 0, l:l + 1], WS, ALU.mult,
                                    ALU.mult).then_inc(s_scaled, 1)

                def merge():
                    dve.wait_ge(s_scaled, l + 1)
                    v.scalar_tensor_tensor(taps, taps, ip2[:, 1, l:l + 1],
                                           win[l][:, None, 0:HID].broadcast_to([128, 9, HID]),
                                           ALU.mult, ALU.mult).then_inc(s_merged, 1)

                def lo_of_projection():
                    dve.wait_ge(s_wh, l + 1)
                    need(dve, s_ready, PLACED * l)
                    v.tensor_tensor(wl[:, :], win[l], wh[:, :], ALU.subtract).then_inc(s_wl, 1)

                def lo_of_taps():
                    dve.wait_ge(s_vh, l + 1)
                    v.tensor_tensor(vl[:, :, :], taps, vh[:, :, :], ALU.subtract).then_inc(s_vl, 1)

                return [scale, merge, lo_of_projection, lo_of_taps]

            def spectra():
                for l in range(LAYERS):
                    dve.wait_ge(s_fold, l + 1)
                    v.tensor_scalar(weff[l][:, :], ps_u[l][:, 0:HID], ip2[:, 1, l:l + 1], 1.0 / (BS * BS * US),
                                    ALU.mult, ALU.mult).then_inc(s_weff, 1)

            for i in range(2):
                v.memset(parts[i][:, :, :, 0:TH], 0.0).then_inc(s_zero, 1)
                v.memset(parts[i][:, :, :, SC - TH:SC], 0.0).then_inc(s_zero, 1)
            for row in (0, H + 1):
                v.memset(x[:, row, :], 0.0)
            for l in range(LAYERS):
                v.memset(pw[l][:, :, :], 0.0).then_inc(s_zero, 1)
            link(v.memset(amax[:, :, :], 0.0))

            def strip_stats(s, it=0):
                for h in range(2):
                    row = 1 + TH * s + TH // 2 * h + 2 * TH * it
                    last = v.bn_stats(st[:, bass.ds(2 * s + h + 4 * it, 1), :].rearrange("p a b -> p (a b)"),
                                      x[:, bass.ds(row, TH // 2), :].rearrange("p r w -> p (r w)"))
                return last

            early = {1: [maxima], 3: [scales], 4: prepare(0)[:2], 5: [spectra], 6: prepare(0)[2:3],
                     7: prepare(0)[3:]}
            for s in range(STRIPS):
                for piece in early.get(s, []):
                    piece()
                dve.wait_ge(s_x[s], 16)
                last = strip_stats(s)
            link(last)
            for l in range(LAYERS):
                base = l * POS
                link(v.bn_aggr(mv[:, :], st[:, :, :].rearrange("p a b -> p (a b)")))
                v.tensor_scalar(ve[:, :], mv[:, 1:2], EPS, None, ALU.add).then_inc(s_var, 1)
                dve.wait_ge(s_root, l + 1)
                link(v.tensor_scalar(nr[:, 1:2], nr[:, 0:1], nr[:, 0:1], ve[:, 0:1], ALU.mult, ALU.mult))
                link(v.tensor_scalar(nr[:, 2:3], nr[:, 1:2], -0.5, 1.5, ALU.mult, ALU.add))
                link(v.tensor_scalar(rstd[:, :], nr[:, 2:3], nr[:, 0:1], XS, ALU.mult, ALU.mult))

                v.tensor_scalar(x[:, H + 1, :], x[:, H + 1, :], 0.0, mv[:, 0:1], ALU.mult, ALU.add)
                link(v.tensor_scalar(x[:, 0, :], x[:, 0, :], 0.0, mv[:, 0:1], ALU.mult, ALU.add))

                def norm(s, it, l=l):
                    need(dve, s_xl, 3 * (l * STRIPS + s - 1 + 2 * it))
                    v.tensor_scalar(xn[:, :, :], x[:, bass.ds(TH * s + 2 * TH * it, TH + 2), :], mv[:, 0:1],
                                    rstd[:, 0:1], ALU.subtract, ALU.mult).then_inc(s_xn, 1)

                def lo_part(s, it, dy, l=l):
                    dve.wait_ge(s_xh, 3 * (l * STRIPS + s + 2 * it) + HI_ORDER.index(dy) + 1)
                    part = parts[s % 2][:, :, 1 + dy, TH:TH + SW].rearrange("p a (w r) -> p a w r", r=TH)
                    v.tensor_tensor(part[:, 1], xn[:, 1 + dy:1 + dy + TH, :].rearrange("p r w -> p w r"),
                                    part[:, 0], ALU.subtract).then_inc(s_xl, 1)

                def copy_groups(s, it, loads, l=l):
                    if s == 0:
                        need(dve, s_s, l * POS - TPS)
                    dve.wait_ge(s_xh, 3 * (l * STRIPS + s + 1 + 2 * it))
                    dve.wait_ge(s_xl, 3 * (l * STRIPS + s + 1 + 2 * it))
                    for load in loads:
                        dst, src = group_ap(s, load)
                        v.tensor_copy(dst, src).then_inc(s_copy, 1)

                norm(0, 0)
                for dy in LO_ORDER:
                    lo_part(0, 0, dy)
                copy_groups(0, 0, FIRST_BY_COPY)
                pieces = prepare(1) if l == 0 else []

                def step(i, it, edge, l=l, base=base, pieces=pieces):
                    n = base + i + UNROLL * it
                    if live(i, -1, edge):
                        k = (i - 1) % 2
                        need(dve, s_s, n)
                        need(dve, s_gelu, n)
                        if l + 1 < LAYERS and i % TPS == 2:
                            need(dve, s_res, n - 2)
                        need(dve, s_ftp, n - 2)
                        v.tensor_tensor(f[:, k, :], ps_s[k][:, 0:GC], g[:, k, :], ALU.mult).then_inc(s_f, 1)
                        if l + 1 < LAYERS and i % TPS == 2 and i > TPS:
                            strip_stats(i // TPS - 1, it)
                    if live(i, 3, edge):
                        k = (i + 3) % 2
                        need(dve, s_uh, n + 4)
                        need(dve, s_z, n + 2)
                        v.scalar_tensor_tensor(ul[:, k, :], ps_u[k][:, 0:GC], US, uh[:, k, :],
                                               ALU.mult, ALU.subtract).then_inc(s_ul, 1)
                    if live(i, 2, edge):
                        k = i % 2
                        need(dve, s_z, n + 3)
                        need(dve, s_yl, n + 1)
                        v.tensor_tensor(y32[:, k, :].rearrange("p (b o) -> p b o", b=B),
                                        ps_z[:, 0:GC].rearrange("p (b o) -> p b o", b=B),
                                        weff[l][:, None, :].broadcast_to([128, B, HID]),
                                        ALU.mult).then_inc(s_y, 1)
                    if live(i, -2, edge):
                        q = i - 2
                        need(dve, s_o, n - 1)
                        xv = x[:, bass.ds(1 + TH * (q // TPS) + 2 * TH * it, TH),
                               TW * (q % TPS):TW * (q % TPS) + TW].rearrange("p r w -> p w r")
                        v.scalar_tensor_tensor(xv, ps_o[:, 0:128].rearrange("p (w r) -> p w r", r=TH),
                                               osc[l][:, 0:1], xv, ALU.mult, ALU.add).then_inc(s_res, 1)
                    s, part = staged(i)
                    if part == 0:
                        norm(s, it)
                    elif part in (2, 3, 4):
                        lo_part(s, it, LO_ORDER[part - 2])
                    s, half = copied(i)
                    if half is not None:
                        copy_groups(s, it, BY_COPY[B * half:B * (half + 1)])
                    if 0 <= i - TAIL < len(pieces):
                        pieces[i - TAIL]()
                schedule(dve, step)
                if l + 1 < LAYERS:
                    dve.wait_ge(s_res, base + POS)
                    link(strip_stats(STRIPS - 1))


def fourier():
    yy, xx = np.meshgrid(np.arange(P), np.arange(P), indexing="ij")
    comps, sources, seen = [], [], set()
    for kh in range(P):
        for kw in range(P // 2 + 1):
            if (kh, kw) in seen:
                continue
            mirror = ((-kh) % P, (-kw) % P)
            seen |= {(kh, kw), mirror}
            theta = 2 * np.pi * (kh * yy + kw * xx) / P
            src = [(kh, kw), mirror] if kw in (0, P // 2) else [(kh, kw)]
            if mirror == (kh, kw):
                comps.append(np.cos(theta) / P)
                sources.append(src[:1])
            else:
                for wave in (np.cos(theta), np.sin(theta)):
                    comps.append(wave * np.sqrt(2) / P)
                    sources.append(src)
    assert len(comps) == P * P
    return np.stack([c.reshape(-1) for c in comps], 1), sources


def constants():
    basis, sources = fourier()
    full = np.zeros((PIX, PIX))
    for pix in range(PIX):
        c, r = divmod(pix, TH)
        full[pix, (c // P) * P * P:(c // P + 1) * P * P] = basis[r * P + c % P]
    full *= BS
    packed = np.zeros((128, 4, 128), np.float16)
    for k, m in enumerate((full, full.T)):
        packed[:, 2 * k] = m.astype(np.float16)
        packed[:, 2 * k + 1] = (m - packed[:, 2 * k].astype(np.float64)).astype(np.float16)
    fold = np.zeros((P * (P // 2 + 1), 128), np.float32)
    for k, src in enumerate(sources):
        for kh, kw in src:
            fold[kh * (P // 2 + 1) + kw, [k, P * P + k]] += 1.0 / len(src)
    return {"basis": packed, "eye32": np.eye(128, dtype=np.float32),
            "fold": fold}


def kernel(**inputs):
    import concourse.bacc as bacc
    from concourse.bass_utils import run_bass_kernel_spmd

    arrays = {"x": np.ascontiguousarray(np.asarray(inputs["x"]).reshape(B * C, H * W))}
    for l in range(LAYERS):
        raw = {k: np.asarray(inputs[f"L{l}_conv_{k}"]) for k in ("W_in", "W_dw", "fft_weight", "W_out")}
        w_in = np.tile(raw["W_in"].T, (B, 1))
        w_dw = np.broadcast_to(raw["W_dw"].reshape(HID, 9).T.reshape(9 * HID), (B * C, 9 * HID))
        arrays[f"w_raw{l}"] = np.ascontiguousarray(np.concatenate([w_in, w_dw], 1))
        arrays[f"w_fft{l}"] = np.ascontiguousarray(raw["fft_weight"].reshape(HID, -1).T)
        arrays[f"w_out{l}"] = np.ascontiguousarray(raw["W_out"].T)
    arrays.update(constants())

    nc = bacc.Bacc("TRN2", target_bir_lowering=False, num_devices=1)
    ap = {k: nc.dram_tensor("in_" + k, a.shape, mybir.dt.from_np(a.dtype), kind="ExternalInput").ap()
          for k, a in arrays.items()}
    y = nc.dram_tensor("out_y", (B * C, H * W), F32, kind="ExternalOutput").ap()
    per_layer = [[ap[f"{k}{l}"] for l in range(LAYERS)] for k in ("w_raw", "w_fft", "w_out")]
    build(nc, ap["x"], *per_layer, ap["basis"], ap["eye32"], ap["fold"], y)
    got = run_bass_kernel_spmd(nc, [{"in_" + k: a for k, a in arrays.items()}], core_ids=[0])
    return got.results[0]["out_y"].reshape(B, C, H, W)
```
